# Optimizing a Trainium2 kernel written in Bass

```python
import numpy as np
import jax
import jax.numpy as jnp

def _softmax(x, axis=-1):
    return jax.nn.softmax(x, axis=axis)

def _gelu(x):
    return jax.nn.gelu(x, approximate=True)

def _silu(x):
    return jax.nn.silu(x)

def _sigmoid(x):
    return jax.nn.sigmoid(x)

def _layernorm(x, axis=-1, eps=1e-05):
    m = jnp.mean(x, axis=axis, keepdims=True)
    v = jnp.var(x, axis=axis, keepdims=True)
    return (x - m) / jnp.sqrt(v + eps)

def _scatter_add(tgt, idx, src, axis=0):
    return tgt.at[idx].add(src)

def _segment_sum(src, seg, n):
    return jax.ops.segment_sum(src, seg, n)
kernel_name = 'mk_seq_postln_d1_jaxref_r8_41ce86'

def setup_inputs(seed: int=0):
    np.random.seed(seed)
    _w = jnp.asarray

    def _L0_attn_setup():
        import jax, jax.numpy as jnp
        import numpy as np
        HEADS = 16
        DIM_HEAD = 64
        B, T, C = (4, 256, 128)

        def apply_rope(x):
            d = x.shape[-1]
            seq_len = x.shape[1]
            inv_freq = 1.0 / 10000.0 ** (jnp.arange(0, d, 2, dtype=jnp.float32) / d)
            pos = jnp.arange(seq_len, dtype=jnp.float32)
            ang = pos[:, None] * inv_freq[None, :]
            sin = jnp.sin(ang)[None]
            cos = jnp.cos(ang)[None]
            x1, x2 = (x[..., 0::2], x[..., 1::2])
            rot = jnp.stack([x1 * cos - x2 * sin, x1 * sin + x2 * cos], axis=-1)
            return rot.reshape(x.shape)
        key = jax.random.key(seed)
        ks = jax.random.split(key, 6)
        inner = HEADS * DIM_HEAD
        w = 0.02
        return {'x': jax.random.normal(ks[0], (B, T, C), dtype=jnp.float32), 'Wq': jax.random.normal(ks[1], (C, inner), dtype=jnp.float32) * w, 'Wk': jax.random.normal(ks[2], (C, inner), dtype=jnp.float32) * w, 'Wv': jax.random.normal(ks[3], (C, inner), dtype=jnp.float32) * w, 'Wo': jax.random.normal(ks[4], (inner, C), dtype=jnp.float32) * w, 'bo': jnp.zeros((C,), dtype=jnp.float32)}
    _L0_attn_in = _L0_attn_setup()

    def _L0_ffn_setup():
        import jax, jax.numpy as jnp
        import numpy as np
        B, S, H, E, K, I = (4, 256, 128, 8, 2, 512)
        GATE_EPS = 1e-06
        LN_EPS = 1e-05
        key = jax.random.key(seed)
        k0, k1, k2, k3 = jax.random.split(key, 4)
        x = jax.random.normal(k0, (B, S, H), jnp.float32)
        gate_w = jax.random.normal(k1, (E, H), jnp.float32) * np.float32(np.sqrt(2.0 / (H + E)))
        expert_bias = jnp.zeros((E,), jnp.float32)
        w_up = jax.random.normal(k2, (E, I, H), jnp.float32) * np.float32(np.sqrt(2.0 / (H + I)))
        w_down = jax.random.normal(k3, (E, H, I), jnp.float32) * np.float32(np.sqrt(2.0 / (H + I)))
        return {'x': x, 'gate_w': gate_w, 'expert_bias': expert_bias, 'w_up': w_up, 'w_down': w_down}
    _L0_ffn_in = _L0_ffn_setup()
    _d = {'L0_attn_x': _L0_attn_in['x'], 'L0_attn_Wq': _L0_attn_in['Wq'], 'L0_attn_Wk': _L0_attn_in['Wk'], 'L0_attn_Wv': _L0_attn_in['Wv'], 'L0_attn_Wo': _L0_attn_in['Wo'], 'L0_attn_bo': _L0_attn_in['bo'], 'L0_ffn_gate_w': _L0_ffn_in['gate_w'], 'L0_ffn_expert_bias': _L0_ffn_in['expert_bias'], 'L0_ffn_w_up': _L0_ffn_in['w_up'], 'L0_ffn_w_down': _L0_ffn_in['w_down']}
    _x0 = _d['L0_attn_x']
    _d['L0_attn_x'] = jax.random.normal(jax.random.fold_in(jax.random.key(seed), 1), (8, 512, 128), dtype=_x0.dtype)
    del _x0
    return _d

def reference(L0_attn_x, L0_attn_Wq, L0_attn_Wk, L0_attn_Wv, L0_attn_Wo, L0_attn_bo, L0_ffn_gate_w, L0_ffn_expert_bias, L0_ffn_w_up, L0_ffn_w_down):

    def _L0_attn_ref(x, Wq, Wk, Wv, Wo, bo):
        import jax, jax.numpy as jnp
        import numpy as np
        HEADS = 16
        DIM_HEAD = 64
        B, T, C = (4, 256, 128)

        def apply_rope(x):
            d = x.shape[-1]
            seq_len = x.shape[1]
            inv_freq = 1.0 / 10000.0 ** (jnp.arange(0, d, 2, dtype=jnp.float32) / d)
            pos = jnp.arange(seq_len, dtype=jnp.float32)
            ang = pos[:, None] * inv_freq[None, :]
            sin = jnp.sin(ang)[None]
            cos = jnp.cos(ang)[None]
            x1, x2 = (x[..., 0::2], x[..., 1::2])
            rot = jnp.stack([x1 * cos - x2 * sin, x1 * sin + x2 * cos], axis=-1)
            return rot.reshape(x.shape)
        b, t, c = x.shape
        h, d = (HEADS, DIM_HEAD)
        scale = d ** (-0.5)

        def split_heads(z):
            return z.reshape(b, t, h, d).transpose(0, 2, 1, 3).reshape(b * h, t, d)
        q = split_heads(x @ Wq)
        k = split_heads(x @ Wk)
        v = split_heads(x @ Wv)
        q = apply_rope(q)
        k = apply_rope(k)
        sim = jnp.einsum('bid,bjd->bij', q, k) * scale
        causal = jnp.tril(jnp.ones((t, t), dtype=bool))
        sim = jnp.where(causal[None], sim, -jnp.inf)
        attn = jax.nn.softmax(sim, axis=-1)
        out = jnp.einsum('bij,bjd->bid', attn, v)
        out = out.reshape(b, h, t, d).transpose(0, 2, 1, 3).reshape(b, t, h * d)
        return out @ Wo + bo

    def _L0_ffn_ref(x, gate_w, expert_bias, w_up, w_down):
        import jax, jax.numpy as jnp
        import numpy as np
        B, S, H, E, K, I = (4, 256, 128, 8, 2, 512)
        GATE_EPS = 1e-06
        LN_EPS = 1e-05
        logits = jnp.einsum('bsh,eh->bse', x, gate_w) + expert_bias
        weights = jax.nn.softmax(logits, axis=-1)
        top_w, top_i = jax.lax.top_k(weights, K)
        top_w = top_w / (jnp.sum(top_w, axis=-1, keepdims=True) + GATE_EPS)
        sparse_w = jnp.sum(jax.nn.one_hot(top_i, E, dtype=weights.dtype) * top_w[..., None], axis=-2)
        out = jnp.zeros_like(x)
        for e in range(E):
            h = jax.nn.gelu(jnp.einsum('bsh,ih->bsi', x, w_up[e]), approximate=False)
            y = jnp.einsum('bsi,hi->bsh', h, w_down[e])
            out = out + sparse_w[..., e:e + 1] * y
        mu = jnp.mean(out, axis=-1, keepdims=True)
        var = jnp.mean(jnp.square(out - mu), axis=-1, keepdims=True)
        out = (out - mu) * jax.lax.rsqrt(var + LN_EPS)
        return out + x
    x = L0_attn_x
    x = _layernorm(x + _L0_attn_ref(x, L0_attn_Wq, L0_attn_Wk, L0_attn_Wv, L0_attn_Wo, L0_attn_bo), axis=-1)
    x = _layernorm(x + _L0_ffn_ref(x, L0_ffn_gate_w, L0_ffn_expert_bias, L0_ffn_w_up, L0_ffn_w_down), axis=-1)
    return x

_drawn_inputs = setup_inputs


def setup_inputs(seed=0):
    import zlib

    import numpy as np

    out = dict(_drawn_inputs(seed))
    spreads = {'L0_attn_bo': (0.0, 0.1), 'L0_ffn_expert_bias': (0.0, 0.1)}
    factors = {'L0_attn_Wq': 8.0, 'L0_attn_Wk': 8.0}
    for name, (base, spread) in spreads.items():
        noise = np.random.default_rng([zlib.crc32(name.encode()), seed]).standard_normal(out[name].shape)
        drawn = base * np.exp(spread * noise) if base else spread * noise
        out[name] = jnp.asarray(drawn.astype(out[name].dtype))
    for name, factor in factors.items():
        out[name] = (out[name] * factor).astype(out[name].dtype)
    return out
```

```python
import concourse.bass as bass
from concourse import mybir
from contextlib import ExitStack

F32 = mybir.dt.float32
ALU = mybir.AluOpType
ACT = mybir.ActivationFunctionType
AX = mybir.AxisListType

P = 128
B, T, C = 8, 512, 128
D = 64
HEADS = 16
PAIRS = HEADS // 2
E, I = 8, 512
QB = T // P
NT = B * QB
IB = I // P
UNITS = B * PAIRS
BLK = 2 * QB
LAG = 3
FUNITS = E * B
LN_EPS = 1e-5
GATE_EPS = 1e-6
NEG = -3.0e38
HUGE = 3.0e38


def build_block(nc, xT_h, x_h, wqkv_h, wo_h, bo_h, cos_h, sin_h, gate_h, ebias_h, wup_h, wdown_h, out_h):
    ctx = ExitStack()
    with ctx:
        def sb(name, shape):
            return ctx.enter_context(nc.sbuf_tensor(name, shape, F32))

        def ps(name):
            return ctx.enter_context(nc.psum_tensor(name, [P, 512], F32))

        def sem(name):
            return ctx.enter_context(nc.semaphore(name))

        ident = sb("ident", [P, P])
        causal = sb("causal", [P, T])
        cos_t = sb("cos_t", [P, T])
        sin_t = sb("sin_t", [P, T])
        bo_t = sb("bo_t", [P, C])
        gate_t = sb("gate_t", [P, E])
        ebias_t = sb("ebias_t", [P, E])
        order = sb("order", [P, E])
        x_acc = sb("x_acc", [P, NT, C])
        f_acc = sb("f_acc", [P, NT, C])
        x1T = sb("x1T", [P, B * T])
        xs = [sb(f"xs{i}", [P, T]) for i in range(2)]
        wqkv = [sb(f"wqkv{i}", [P, 3 * P]) for i in range(2)]
        wo = [sb(f"wo{i}", [P, C]) for i in range(2)]
        qT = [sb(f"qT{i}", [P, T]) for i in range(2)]
        kM = [sb(f"kM{i}", [P, 2, T]) for i in range(2)]
        V = [sb(f"V{i}", [P, QB, P]) for i in range(2)]
        PT = [sb(f"PT{i}", [P, 2, QB, T]) for i in range(2)]
        OT = [sb(f"OT{i}", [P, T]) for i in range(2)]
        Sm = [sb(f"Sm{i}", [P, T]) for i in range(2)]
        Pr = [sb(f"Pr{i}", [P, T]) for i in range(4)]
        q_cos, q_rot, k_cos, k_rot = (sb(n, [P, T]) for n in ("q_cos", "q_rot", "k_cos", "k_rot"))
        nmax = sb("nmax", [P, BLK])
        rsum = sb("rsum", [P, BLK])
        rinv = sb("rinv", [P, BLK])
        wu = [sb(f"wu{i}", [P, I]) for i in range(2)]
        wd = [sb(f"wd{i}", [P, IB, C]) for i in range(2)]
        hT = [sb(f"hT{i}", [P, IB, T]) for i in range(2)]
        st = sb("st", [P, NT, 6])
        mv = sb("mv", [P, NT, 2])
        sd = sb("sd", [P, NT])
        rstd = sb("rstd", [P, NT])
        lg = sb("lg", [P, NT, E])
        wt = sb("wt", [P, NT, E])
        w2 = sb("w2", [P, NT, E])
        c1 = sb("c1", [P, NT, E])
        k1 = sb("k1", [P, NT, E])
        m1 = sb("m1", [P, NT])
        m2 = sb("m2", [P, NT])
        s1 = sb("s1", [P, NT])
        spw = sb("spw", [P, NT, E])

        SB = [ps("SB0"), ps("SB1")]
        TB = [ps("TB0"), ps("TB1")]
        QP, KP = ps("QP"), ps("KP")
        OB, YB = ps("OB"), ps("YB")
        HB = [SB[0], SB[1], QP, KP]
        FB = [OB, YB]

        consts_in = sem("consts_in")
        x_in = sem("x_in")
        xw_in = [sem("xw_in0"), sem("xw_in1")]
        wo_in = [sem("wo_in0"), sem("wo_in1")]
        pool_set = sem("pool_set")
        q_proj, k_proj, v_proj = sem("q_proj"), sem("k_proj"), sem("v_proj")
        q_read, k_read = sem("q_read"), sem("k_read")
        q_mul, k_mul = sem("q_mul"), sem("k_mul")
        q_ready, k_ready, v_ready = sem("q_ready"), sem("k_ready"), sem("v_ready")
        scored = sem("scored")
        maxed = sem("maxed")
        exped = sem("exped")
        inverted = sem("inverted")
        normed = sem("normed")
        transposed = sem("transposed")
        pt_ready = sem("pt_ready")
        pv_done = sem("pv_done")
        o_ready = sem("o_ready")
        y_done = sem("y_done")
        y_added = sem("y_added")
        x_set = sem("x_set")
        chain = sem("chain")
        var_ready, sd_ready = sem("var_ready"), sem("sd_ready")
        x1_ready = sem("x1_ready")
        x1_tr, x1T_ready = sem("x1_tr"), sem("x1T_ready")
        logits_done = sem("logits_done")
        gate_sub, gate_exp = sem("gate_sub"), sem("gate_exp")
        w_in = [sem("w_in0"), sem("w_in1")]
        up_done, gelu_done = sem("up_done"), sem("gelu_done")
        down_done, f_added = sem("down_done"), sem("f_added")
        out_ready, out_sent = sem("out_ready"), sem("out_sent")

        block = ctx.enter_context(nc.Block())

        def wait(eng, semaphore, count):
            if not isinstance(count, int) or count > 0:
                eng.wait_ge(semaphore, count)

        def units(eng, count, emit):
            emit(0, 0, True, False)
            emit(1, 1, False, False)
            with eng.Fori(1, count // 2 - 1) as t:
                emit(2 * t, 0, False, False)
                emit(2 * t + 1, 1, False, False)
            emit(count - 2, 0, False, False)
            emit(count - 1, 1, False, True)

        @block.sync
        def _(sp):
            def load_xw(u, p):
                if p is None:
                    return
                wait(sp, v_proj, u - 1)
                batch, pair = u // PAIRS, u % PAIRS
                sp.dma_start(xs[p][:, :], xT_h[:, bass.ds(batch * T, T)]).then_inc(xw_in[p], 16)
                sp.dma_start(wqkv[p][:, :], wqkv_h[bass.ds(pair, 1), :, :].rearrange("a c n -> c (a n)")).then_inc(xw_in[p], 16)

            def attention_loads(u, p, first, last):
                if first:
                    load_xw(0, 0)
                    for dst, src in ((cos_t, cos_h), (sin_t, sin_h), (bo_t, bo_h), (gate_t, gate_h), (ebias_t, ebias_h)):
                        sp.dma_start(dst[:, :], src).then_inc(consts_in, 16)
                    sp.dma_start(x_acc[:, :, :], x_h.rearrange("(t p) c -> p t c", p=P)).then_inc(x_in, 16)
                if not last:
                    load_xw(u + 1, 1 - p)
                wait(sp, y_done, u - 1)
                sp.dma_start(wo[p][:, :], wo_h[bass.ds((u % PAIRS) * P, P), :]).then_inc(wo_in[p], 16)

            units(sp, UNITS, attention_loads)

            def ffn_loads(v, p, first, last):
                wait(sp, down_done, v - 1)
                e = v // B
                sp.dma_start(wu[p][:, :], wup_h[:, bass.ds(e * I, I)]).then_inc(w_in[p], 16)
                sp.dma_start(wd[p][:, :, :], wdown_h[:, bass.ds(e * IB, IB), :]).then_inc(w_in[p], 16)

            units(sp, FUNITS, ffn_loads)
            out_v = out_h.rearrange("(t p) c -> p t c", p=P)
            for b in range(B):
                sp.wait_ge(out_ready, b + 1)
                sp.dma_start(out_v[:, QB * b:QB * b + QB, :], f_acc[:, QB * b:QB * b + QB, :]).then_inc(out_sent, 16)
            sp.wait_ge(out_sent, 16 * B)

        @block.gpsimd
        def _(pool):
            for p in range(2):
                nc.gpsimd.memset(kM[p][:, :, :], 0.0).then_inc(pool_set, 1)
            nc.gpsimd.memset(ident[:, :], 0.0).then_inc(pool_set, 1)
            nc.gpsimd.memset(causal[:, :], 0.0).then_inc(pool_set, 1)
            nc.gpsimd.iota(order[:, :], pattern=[[-1, E]], base=E, channel_multiplier=0,
                           allow_small_or_imprecise_dtypes=True).then_inc(pool_set, 1)
            pool.wait_ge(pool_set, 5)
            nc.gpsimd.affine_select(out=ident[:, :], in_=ident[:, :], compare_op=ALU.not_equal, fill=1.0,
                                    base=0, pattern=[[-1, P]], channel_multiplier=1).then_inc(pool_set, 1)
            nc.gpsimd.affine_select(out=causal[:, T - P:T], in_=causal[:, T - P:T], compare_op=ALU.is_ge, fill=NEG,
                                    base=0, pattern=[[-1, P]], channel_multiplier=1).then_inc(pool_set, 1)
            pool.wait_ge(consts_in, 16 * 5)

            def rotate(u, p, first, last):
                pool.wait_ge(q_read, u + 1)
                nc.gpsimd.tensor_tensor(q_rot[:, :], q_rot[:, :], sin_t[:, :], ALU.mult).then_inc(q_mul, 1)
                wait(pool, scored, BLK * (u - 1))
                pool.wait_ge(q_mul, u + 1)
                nc.gpsimd.tensor_tensor(qT[p][:, :], q_cos[:, :], q_rot[:, :], ALU.add).then_inc(q_ready, 1)
                pool.wait_ge(k_read, u + 1)
                nc.gpsimd.tensor_tensor(k_rot[:, :], k_rot[:, :], sin_t[:, :], ALU.mult).then_inc(k_mul, 1)
                pool.wait_ge(k_mul, u + 1)
                for h in range(2):
                    half = slice(D * h, D * h + D)
                    nc.gpsimd.tensor_tensor(kM[p][half, h, :], k_cos[half, :], k_rot[half, :], ALU.add).then_inc(k_ready, 1)

            units(pool, UNITS, rotate)

        @block.tensor
        def _(pe):
            def project_qk(u, p):
                pe.wait_ge(xw_in[p], 32 * (u // 2 + 1))
                wait(pe, v_ready, u)
                nc.tensor.matmul(QP[:, :], wqkv[p][:, 0:P], xs[p][:, :], start=True, stop=True).then_inc(q_proj, 1)
                wait(pe, k_read, u)
                nc.tensor.matmul(KP[:, :], wqkv[p][:, P:2 * P], xs[p][:, :], start=True, stop=True).then_inc(k_proj, 1)

            def project_v(u, p):
                pe.wait_ge(q_read, u + 1)
                for kb in range(QB):
                    last = nc.tensor.matmul(QP[:, kb * P:kb * P + P], xs[p][:, kb * P:kb * P + P],
                                            wqkv[p][:, 2 * P:3 * P], start=True, stop=True)
                last.then_inc(v_proj, 1)

            def score(u, p, j):
                g, h, qb = BLK * u + j, j // QB, j % QB
                wait(pe, maxed, g - 1)
                nc.tensor.matmul(SB[j % 2][:, 0:(qb + 1) * P], qT[p][:, qb * P:qb * P + P], kM[p][:, h, 0:(qb + 1) * P],
                                 start=True, stop=True).then_inc(scored, 1)

            def transpose(u, p, j):
                g, qb = BLK * u + j, j % QB
                pe.wait_ge(normed, g + 1)
                wait(pe, pt_ready, g - 1)
                for kb in range(qb + 1):
                    last = nc.tensor.transpose(TB[j % 2][:, kb * P:kb * P + P], Pr[j % 4][:, kb * P:kb * P + P], ident[:, :])
                last.then_inc(transposed, 1)

            def attend(u, p):
                pe.wait_ge(pt_ready, BLK * (u + 1))
                pe.wait_ge(v_ready, u + 1)
                wait(pe, o_ready, u)
                for kb in range(QB):
                    for h in range(2):
                        last = nc.tensor.matmul(OB[D * h:D * h + D, kb * P:T], V[p][:, kb, D * h:D * h + D],
                                                PT[p][:, h, kb, kb * P:T], start=(kb == 0), stop=(kb == QB - 1))
                last.then_inc(pv_done, 1)

            def project_out(u, p):
                pe.wait_ge(wo_in[p], 16 * (u // 2 + 1))
                pe.wait_ge(o_ready, u + 1)
                wait(pe, y_added, u)
                for i in range(QB):
                    last = nc.tensor.matmul(YB[:, i * P:i * P + P], OT[p][:, i * P:i * P + P], wo[p][:, :],
                                            start=True, stop=True)
                last.then_inc(y_done, 1)

            def attention(u, p, first, last):
                if first:
                    project_qk(0, 0)
                    project_v(0, 0)
                    pe.wait_ge(pool_set, 7)
                pe.wait_ge(q_ready, u + 1)
                pe.wait_ge(k_ready, 2 * u + 2)
                for j in range(BLK):
                    score(u, p, j)
                    if j >= LAG:
                        transpose(u, p, j - LAG)
                    elif not first:
                        transpose(u - 1, 1 - p, BLK + j - LAG)
                    if j == 2 and not last:
                        project_qk(u + 1, 1 - p)
                    if j == 4 and not first:
                        attend(u - 1, 1 - p)
                    if j == 6 and not last:
                        project_v(u + 1, 1 - p)
                    if j == 7 and not first:
                        project_out(u - 1, 1 - p)

            units(pe, UNITS, attention)
            u = UNITS - 1
            for j in range(BLK - LAG, BLK):
                transpose(u, 1, j)
            attend(u, 1)
            project_out(u, 1)

            pe.wait_ge(y_added, UNITS)
            pe.wait_ge(consts_in, 16 * 5)
            for b in range(B):
                pe.wait_ge(x1_ready, b + 1)
                wait(pe, x1T_ready, b - 1)
                for i in range(QB):
                    last = nc.tensor.transpose(TB[b % 2][:, i * P:i * P + P], x_acc[:, QB * b + i, :], ident[:, :])
                last.then_inc(x1_tr, 1)
            for b in range(B):
                pe.wait_ge(x1T_ready, b + 1)
                for i in range(QB):
                    n = QB * b + i
                    last = nc.tensor.matmul(KP[:, n * E:n * E + E], x1T[:, n * P:n * P + P], gate_t[:, :],
                                            start=True, stop=True)
                last.then_inc(logits_done, 1)

            def up(v, p, ib, b):
                w = IB * v + ib
                wait(pe, gelu_done, w + 1 - IB)
                nc.tensor.matmul(HB[ib][:, :], wu[p][:, ib * P:ib * P + P], x1T[:, bass.ds(b * T, T)],
                                 start=True, stop=True).then_inc(up_done, 1)

            def down(v, p, i):
                for ib in range(IB):
                    last = nc.tensor.matmul(FB[p][:, i * P:i * P + P], hT[p][:, ib, i * P:i * P + P], wd[p][:, ib, :],
                                            start=(ib == 0), stop=(ib == IB - 1))
                if i == QB - 1:
                    last.then_inc(down_done, 1)

            def down_waits(v, p):
                pe.wait_ge(gelu_done, IB * (v + 1))
                wait(pe, f_added, QB * (v - 1))

            def ffn(v, p, first, last):
                if first:
                    pe.wait_ge(gate_sub, 1)
                pe.wait_ge(w_in[p], 32 * (v // 2 + 1))
                for ib in range(IB):
                    up(v, p, ib, v % B)
                    if not first:
                        if ib == 0:
                            down_waits(v - 1, 1 - p)
                        down(v - 1, 1 - p, ib)

            units(pe, FUNITS, ffn)
            down_waits(FUNITS - 1, 1)
            for i in range(QB):
                down(FUNITS - 1, 1, i)

        @block.scalar
        def _(act):
            def copy_v(u, p):
                act.wait_ge(v_proj, u + 1)
                nc.scalar.activation(V[p][:, :, :], QP[:, :].rearrange("k (b f) -> k b f", b=QB), ACT.Copy).then_inc(v_ready, 1)

            def exp(u, p, j):
                g, qb = BLK * u + j, j % QB
                act.wait_ge(maxed, g + 1)
                wait(act, transposed, g - 3)
                n = (qb + 1) * P
                nc.scalar.activation(Pr[j % 4][:, 0:n], Sm[j % 2][:, 0:n], ACT.Exp, bias=nmax[:, j:j + 1], scale=-1.0,
                                     accum_out=rsum[:, j:j + 1]).then_inc(exped, 1)

            def copy_pt(u, p, j):
                h, qb = j // QB, j % QB
                act.wait_ge(transposed, BLK * u + j + 1)
                nc.scalar.activation(PT[p][:, h, 0:qb + 1, qb * P:qb * P + P],
                                     TB[j % 2][:, 0:(qb + 1) * P].rearrange("k (b q) -> k b q", q=P),
                                     ACT.Copy).then_inc(pt_ready, 1)

            def copy_o(u, p):
                act.wait_ge(pv_done, u + 1)
                nc.scalar.activation(OT[p][:, :], OB[:, :], ACT.Copy).then_inc(o_ready, 1)

            def attention(u, p, first, last):
                if first:
                    copy_v(0, 0)
                for j in range(BLK):
                    exp(u, p, j)
                    if j >= LAG:
                        copy_pt(u, p, j - LAG)
                    elif not first:
                        copy_pt(u - 1, 1 - p, BLK + j - LAG)
                    if j == 5 and not first:
                        copy_o(u - 1, 1 - p)
                    if j == 7 and not last:
                        copy_v(u + 1, 1 - p)

            units(act, UNITS, attention)
            u = UNITS - 1
            for j in range(BLK - LAG, BLK):
                copy_pt(u, 1, j)
            copy_o(u, 1)

            act.wait_ge(var_ready, 1)
            nc.scalar.activation(sd[:, :], mv[:, :, 1], ACT.Sqrt).then_inc(sd_ready, 1)
            for b in range(B):
                act.wait_ge(x1_tr, b + 1)
                nc.scalar.activation(x1T[:, b * T:b * T + T], TB[b % 2][:, :], ACT.Copy).then_inc(x1T_ready, 1)
            act.wait_ge(gate_sub, 1)
            nc.scalar.activation(wt[:, :, :], lg[:, :, :], ACT.Exp).then_inc(gate_exp, 1)

            def ffn(v, p, first, last):
                for ib in range(IB):
                    act.wait_ge(up_done, IB * v + ib + 1)
                    if ib == 0:
                        wait(act, down_done, v - 1)
                    nc.scalar.activation(hT[p][:, ib, :], HB[ib][:, :], ACT.Gelu).then_inc(gelu_done, 1)

            units(act, FUNITS, ffn)
            for n in (2, 3):
                act.wait_ge(var_ready, n)
                nc.scalar.activation(sd[:, :], mv[:, :, 1], ACT.Sqrt).then_inc(sd_ready, 1)

        @block.vector
        def _(dve):
            steps = [0]

            def done(ins):
                steps[0] += 1
                ins.then_inc(chain, 1)
                dve.wait_ge(chain, steps[0])

            swap = [i ^ 1 for i in range(32)]

            def rope_q(u):
                dve.wait_ge(q_proj, u + 1)
                wait(dve, q_ready, u)
                nc.vector.tensor_tensor(q_cos[:, :], QP[:, :], cos_t[:, :], ALU.mult)
                nc.vector.stream_shuffle(q_rot[:, :], QP[:, :], swap).then_inc(q_read, 1)

            def rope_k(u):
                dve.wait_ge(k_proj, u + 1)
                wait(dve, k_ready, 2 * u)
                nc.vector.tensor_tensor(k_cos[:, :], KP[:, :], cos_t[:, :], ALU.mult)
                nc.vector.stream_shuffle(k_rot[:, :], KP[:, :], swap).then_inc(k_read, 1)

            def mask_max(u, j):
                n = (j % QB + 1) * P
                nc.vector.tensor_tensor_reduce(out=Sm[j % 2][:, 0:n], in0=SB[j % 2][:, 0:n], in1=causal[:, T - n:T],
                                               scale=-0.125, scalar=HUGE, op0=ALU.add, op1=ALU.min,
                                               accum_out=nmax[:, j:j + 1]).then_inc(maxed, 1)

            def invert(u, j):
                dve.wait_ge(exped, BLK * u + j + 1)
                nc.vector.reciprocal(rinv[:, j:j + 1], rsum[:, j:j + 1]).then_inc(inverted, 1)

            def norm(u, j):
                n = (j % QB + 1) * P
                dve.wait_ge(inverted, BLK * u + j + 1)
                nc.vector.tensor_scalar(Pr[j % 4][:, 0:n], Pr[j % 4][:, 0:n], rinv[:, j:j + 1], None,
                                        ALU.mult).then_inc(normed, 1)

            def add_y(u):
                b = u // PAIRS
                tiles = x_acc[:, bass.ds(b * QB, QB), :]
                dve.wait_ge(y_done, u + 1)
                wait(dve, y_added, u)
                nc.vector.tensor_tensor(tiles, YB[:, :].rearrange("t (b c) -> t b c", b=QB), tiles,
                                        ALU.add).then_inc(y_added, 1)

            def attention(u, p, first, last):
                if first:
                    dve.wait_ge(consts_in, 16 * 5)
                    rope_q(0)
                    rope_k(0)
                    dve.wait_ge(x_in, 16)
                    done(nc.vector.tensor_tensor(x_acc[:, :, :], x_acc[:, :, :],
                                                 bo_t[:, :].unsqueeze(1).to_broadcast([P, NT, C]), ALU.add))
                    done(nc.vector.memset(f_acc[:, :, :], 0.0))
                    dve.wait_ge(pool_set, 7)
                for j in range(BLK):
                    dve.wait_ge(scored, BLK * u + j + 1)
                    before = (u, j - 2) if j >= 2 else None if first else (u - 1, BLK + j - 2)
                    if before:
                        invert(*before)
                    mask_max(u, j)
                    if before:
                        norm(*before)
                    if j == 3 and not last:
                        rope_q(u + 1)
                    if j == 4 and not last:
                        rope_k(u + 1)
                    if j == 2 and not first:
                        if not isinstance(u, int) or u > 1:
                            add_y(u - 2)

            units(dve, UNITS, attention)
            for j in (BLK - 2, BLK - 1):
                invert(UNITS - 1, j)
                norm(UNITS - 1, j)
            add_y(UNITS - 2)
            add_y(UNITS - 1)
            dve.wait_ge(y_added, UNITS)

            def statistics(src, eps, n):
                for i in range(NT):
                    last = nc.vector.bn_stats(st[:, i, :], src[:, i, :])
                done(last)
                for i in range(NT):
                    last = nc.vector.bn_aggr(mv[:, i, :], st[:, i, :])
                done(last)
                nc.vector.tensor_scalar(mv[:, :, 1], mv[:, :, 1], eps, None, ALU.add).then_inc(var_ready, 1)
                dve.wait_ge(sd_ready, n)
                done(nc.vector.reciprocal(rstd[:, :], sd[:, :]))

            statistics(x_acc, LN_EPS, 1)
            for i in range(NT):
                last = nc.vector.tensor_scalar(x_acc[:, i, :], x_acc[:, i, :], mv[:, i, 0:1], rstd[:, i:i + 1],
                                               ALU.subtract, ALU.mult)
                if i % QB == QB - 1:
                    last.then_inc(x1_ready, 1)

            def over_e(t):
                return t[:, :].unsqueeze(2).to_broadcast([P, NT, E])

            def over_t(t):
                return t[:, :].unsqueeze(1).to_broadcast([P, NT, E])

            dve.wait_ge(logits_done, B)
            done(nc.vector.tensor_tensor(lg[:, :, :], KP[:, 0:NT * E].rearrange("p (n e) -> p n e", e=E), over_t(ebias_t), ALU.add))
            done(nc.vector.tensor_reduce(m1[:, :], lg[:, :, :], AX.X, ALU.max))
            nc.vector.tensor_tensor(lg[:, :, :], lg[:, :, :], over_e(m1), ALU.subtract).then_inc(gate_sub, 1)
            dve.wait_ge(gate_exp, 1)
            done(nc.vector.tensor_reduce(s1[:, :], wt[:, :, :], AX.X, ALU.add))
            done(nc.vector.reciprocal(s1[:, :], s1[:, :]))
            done(nc.vector.tensor_tensor(wt[:, :, :], wt[:, :, :], over_e(s1), ALU.mult))

            def pick(weights, best, chosen):
                done(nc.vector.tensor_reduce(best[:, :], weights[:, :, :], AX.X, ALU.max))
                done(nc.vector.tensor_tensor(chosen[:, :, :], weights[:, :, :], over_e(best), ALU.is_equal))
                done(nc.vector.tensor_tensor(chosen[:, :, :], chosen[:, :, :], over_t(order), ALU.mult))
                done(nc.vector.tensor_reduce(s1[:, :], chosen[:, :, :], AX.X, ALU.max))
                done(nc.vector.tensor_tensor(chosen[:, :, :], chosen[:, :, :], over_e(s1), ALU.is_equal))

            pick(wt, m1, c1)
            done(nc.vector.scalar_tensor_tensor(out=w2[:, :, :], in0=c1[:, :, :], scalar=-2.0, in1=wt[:, :, :],
                                                op0=ALU.mult, op1=ALU.add))
            pick(w2, m2, k1)
            done(nc.vector.tensor_tensor(c1[:, :, :], c1[:, :, :], k1[:, :, :], ALU.add))
            done(nc.vector.scalar_tensor_tensor(out=m1[:, :], in0=m1[:, :], scalar=GATE_EPS, in1=m2[:, :],
                                                op0=ALU.add, op1=ALU.add))
            done(nc.vector.reciprocal(m1[:, :], m1[:, :]))
            done(nc.vector.tensor_tensor(wt[:, :, :], wt[:, :, :], c1[:, :, :], ALU.mult))
            done(nc.vector.tensor_tensor(spw[:, :, :], wt[:, :, :], over_e(m1), ALU.mult))

            def ffn(v, p, first, last):
                e, b = v // B, v % B
                dve.wait_ge(down_done, v + 1)
                for i in range(QB):
                    tile = f_acc[:, bass.ds(b * QB + i, 1), :].rearrange("p a c -> p (a c)")
                    weight = spw[:, bass.ds(b * QB + i, 1), bass.ds(e, 1)].rearrange("p a c -> p (a c)")
                    nc.vector.scalar_tensor_tensor(out=tile, in0=FB[p][:, i * P:i * P + P], scalar=weight, in1=tile,
                                                   op0=ALU.mult, op1=ALU.add).then_inc(f_added, 1)

            units(dve, FUNITS, ffn)
            dve.wait_ge(f_added, QB * FUNITS)
            statistics(f_acc, LN_EPS, 2)
            for i in range(NT):
                last = nc.vector.tensor_scalar(f_acc[:, i, :], f_acc[:, i, :], mv[:, i, 0:1], rstd[:, i:i + 1],
                                               ALU.subtract, ALU.mult)
            done(last)
            done(nc.vector.tensor_tensor(f_acc[:, :, :], f_acc[:, :, :], x_acc[:, :, :], ALU.add))
            done(nc.vector.tensor_tensor(f_acc[:, :, :], f_acc[:, :, :], x_acc[:, :, :], ALU.add))
            statistics(f_acc, LN_EPS, 3)
            for i in range(NT):
                last = nc.vector.tensor_scalar(f_acc[:, i, :], f_acc[:, i, :], mv[:, i, 0:1], rstd[:, i:i + 1],
                                               ALU.subtract, ALU.mult)
                if i % QB == QB - 1:
                    last.then_inc(out_ready, 1)


def rope_tables():
    import numpy as np
    inv_freq = (np.float32(1.0) / np.float32(10000.0) ** (np.arange(0, D, 2, dtype=np.float32) / np.float32(D))).astype(np.float32)
    ang = (np.arange(T, dtype=np.float32)[None, :] * inv_freq[:, None]).astype(np.float32)
    sign = np.array([-1.0, 1.0], np.float32)[:, None]
    cos = np.tile(np.repeat(np.cos(ang), 2, axis=0), (2, 1))
    sin = np.tile((np.sin(ang)[:, None, :] * sign).reshape(D, T), (2, 1))
    return np.ascontiguousarray(cos, np.float32), np.ascontiguousarray(sin, np.float32)


def kernel(**inputs):
    import numpy as np
    import concourse.bacc as bacc
    from concourse.bass_utils import run_bass_kernel_spmd

    a = {k.replace("L0_", ""): np.asarray(v) for k, v in inputs.items()}
    cos, sin = rope_tables()
    x = a["attn_x"].reshape(B * T, C)
    qkv = [a[f"attn_W{n}"].reshape(C, PAIRS, P).transpose(1, 0, 2) for n in "qkv"]
    arrays = {
        "xT": x.T,
        "x": x,
        "wqkv": np.concatenate(qkv, axis=2),
        "wo": a["attn_Wo"],
        "bo": np.broadcast_to(a["attn_bo"], (P, C)),
        "cos": cos,
        "sin": sin,
        "gate": a["ffn_gate_w"].T,
        "ebias": np.broadcast_to(a["ffn_expert_bias"], (P, E)),
        "wup": a["ffn_w_up"].reshape(E * I, C).T,
        "wdown": a["ffn_w_down"].reshape(E, C, IB, P).transpose(3, 0, 2, 1).reshape(P, E * IB, C),
    }
    arrays = {f"in_{k}": np.ascontiguousarray(v) for k, v in arrays.items()}
    nc = bacc.Bacc("TRN2", target_bir_lowering=False, num_devices=1)
    args = [nc.dram_tensor(k, v.shape, mybir.dt.from_np(v.dtype), kind="ExternalInput").ap() for k, v in arrays.items()]
    out = nc.dram_tensor("out_0", (B * T, C), F32, kind="ExternalOutput").ap()
    build_block(nc, *args, out)
    r = run_bass_kernel_spmd(nc, [arrays], core_ids=[0])
    return r.results[0]["out_0"].reshape(B, T, C)
```

```python
import concourse.bass as bass
from concourse import mybir
from contextlib import ExitStack

F32 = mybir.dt.float32
ALU = mybir.AluOpType
ACT = mybir.ActivationFunctionType
AX = mybir.AxisListType

P = 128
B, T, C = 8, 512, 128
D = 64
HEADS = 16
PAIRS = HEADS // 2
E, I = 8, 512
QB = T // P
NT = B * QB
IB = I // P
UNITS = B * PAIRS
BLK = 2 * QB
LAG = 3
K = 2
TILES = (B * T * K + E * (P - 1)) // P + 1
TILES += -TILES % 4
REGION = B * T + P
SPARE = E * REGION
Y0 = TILES * P
ROW = C + 2
XT = 4
LN_EPS = 1e-5
ROUTE = 26
POOL_SET = 16
MAGIC = 1.5 * 2.0 ** 23
I32 = mybir.dt.int32
GATE_EPS = 1e-6
NEG = -3.0e38
HUGE = 3.0e38


def build_block(nc, xT_h, x_h, wqkv_h, wo_h, bo_h, cos_h, sin_h, gate_h, ebias_h, wup_h, wdown_h, xrows, yrows, out_h):
    ctx = ExitStack()
    with ctx:
        def sb(name, shape, dtype=F32):
            return ctx.enter_context(nc.sbuf_tensor(name, shape, dtype))

        def ps(name):
            return ctx.enter_context(nc.psum_tensor(name, [P, 512], F32))

        def sem(name):
            return ctx.enter_context(nc.semaphore(name))

        ident = sb("ident", [P, P])
        causal = sb("causal", [P, T])
        cos_t = sb("cos_t", [P, T])
        sin_t = sb("sin_t", [P, T])
        bo_t = sb("bo_t", [P, C])
        gate_t = sb("gate_t", [P, E])
        ebias_t = sb("ebias_t", [P, E])
        order = sb("order", [P, E])
        before_t = sb("before_t", [P, P])
        ones_t = sb("ones_t", [P, P])
        row_id = sb("row_id", [P, NT, K])
        pad_id = sb("pad_id", [P, TILES])
        tile_no = sb("tile_no", [1, TILES])
        part_no = sb("part_no", [P, 1])
        eps_t = sb("eps_t", [P, 1])
        region = sb("region", [P, E])
        pad_row = sb("pad_row", [P, ROW])
        x_acc = sb("x_acc", [P, NT, C])
        f_acc = sb("f_acc", [P, NT, C])
        xs = [sb(f"xs{i}", [P, T]) for i in range(2)]
        wqkv = [sb(f"wqkv{i}", [P, 3 * P]) for i in range(2)]
        wo = [sb(f"wo{i}", [P, C]) for i in range(2)]
        qT = [sb(f"qT{i}", [P, T]) for i in range(2)]
        kM = [sb(f"kM{i}", [P, 2, T]) for i in range(2)]
        V = [sb(f"V{i}", [P, QB, P]) for i in range(2)]
        PT = [sb(f"PT{i}", [P, 2, QB, T]) for i in range(2)]
        OT = [sb(f"OT{i}", [P, T]) for i in range(2)]
        Sm = [sb(f"Sm{i}", [P, T]) for i in range(2)]
        Pr = [sb(f"Pr{i}", [P, T]) for i in range(4)]
        q_cos, q_rot, k_cos, k_rot = (sb(n, [P, T]) for n in ("q_cos", "q_rot", "k_cos", "k_rot"))
        nmax = sb("nmax", [P, BLK])
        rsum = sb("rsum", [P, BLK])
        rinv = sb("rinv", [P, BLK])
        st = sb("st", [P, QB, 6])
        mv = sb("mv", [P, QB, 2])
        sd = sb("sd", [P, QB])
        rstd = sb("rstd", [P, QB])
        x1T = sb("x1T", [P, T])
        lg, wt, w2, c1, c2, cc, slots_f = (sb(n, [P, QB, E]) for n in ("lg", "wt", "w2", "c1", "c2", "cc", "slots_f"))
        m1, m2, s1, den = (sb(n, [P, QB]) for n in ("m1", "m2", "s1", "den"))
        before_n = sb("before_n", [P, QB, E])
        next_row = sb("next_row", [P, E])
        slot_f = sb("slot_f", [P, QB, K])
        slot = sb("slot", [P, QB, K], I32)
        pay = sb("pay", [P, QB, K, ROW])
        count = sb("count", [P, E])
        tiles_of = sb("tiles_of", [P, E])
        start = sb("start", [P, E + 1])
        past = sb("past", [1, TILES, E])
        exp_f, row_f, ok_f = (sb(n, [1, TILES]) for n in ("exp_f", "row_f", "ok_f"))
        tile_expert = sb("tile_expert", [1, TILES], I32)
        tile_row = sb("tile_row", [1, TILES], I32)
        pad_f = sb("pad_f", [P, E])
        pad_slot = sb("pad_slot", [P, E], I32)
        wup = sb("wup", [P, E * I])
        wdown = sb("wdown", [P, E * IB, C])
        xt = [sb(f"xt{i}", [P, ROW]) for i in range(XT)]
        xT = [sb(f"xT{i}", [P, P]) for i in range(2)]
        hid = [sb(f"hid{i}", [P, I]) for i in range(2)]
        hT = [sb(f"hT{i}", [P, I]) for i in range(2)]
        ys = [sb(f"ys{i}", [P, C]) for i in range(XT)]
        y_row = [sb(f"y_row{i}", [P, 1], I32) for i in range(XT)]
        y_weight = [sb(f"y_weight{i}", [P, 1]) for i in range(XT)]
        st2 = sb("st2", [P, NT, 6])
        mv2 = sb("mv2", [P, 2, NT, 2])
        sd2 = sb("sd2", [P, 2, NT])
        rstd2 = sb("rstd2", [P, 2, NT])

        SB = [ps("SB0"), ps("SB1")]
        TB = [ps("TB0"), ps("TB1")]
        QP, KP = ps("QP"), ps("KP")
        OB, YB = ps("OB"), ps("YB")
        XB, HB, GB, FB = [QP, KP], SB, TB, [OB, YB]

        consts_in = sem("consts_in")
        x_in = sem("x_in")
        xw_in = [sem("xw_in0"), sem("xw_in1")]
        wo_in = [sem("wo_in0"), sem("wo_in1")]
        pool_set = sem("pool_set")
        q_proj, k_proj, v_proj = sem("q_proj"), sem("k_proj"), sem("v_proj")
        q_read, k_read = sem("q_read"), sem("k_read")
        q_mul, k_mul = sem("q_mul"), sem("k_mul")
        q_ready, k_ready, v_ready = sem("q_ready"), sem("k_ready"), sem("v_ready")
        scored = sem("scored")
        maxed = sem("maxed")
        exped = sem("exped")
        inverted = sem("inverted")
        normed = sem("normed")
        transposed = sem("transposed")
        pt_ready = sem("pt_ready")
        pv_done = sem("pv_done")
        o_ready = sem("o_ready")
        y_done = sem("y_done")
        y_added = sem("y_added")
        x_set = sem("x_set")
        chain = sem("chain")
        eps_set = sem("eps_set")
        route_step = sem("route_step")
        stats_done = sem("stats_done")
        x1_kept = sem("x1_kept")
        var_ready, sd_ready = sem("var_ready"), sem("sd_ready")
        x1_ready = sem("x1_ready")
        x1_tr, x1T_ready = sem("x1_tr"), sem("x1T_ready")
        pay_ready = sem("pay_ready")
        logits_done = sem("logits_done")
        gate_sub, gate_exp = sem("gate_sub"), sem("gate_exp")
        chosen, ranked = sem("chosen"), sem("ranked")
        slots_ready = sem("slots_ready")
        rows_sent = sem("rows_sent")
        pad_set, pads_ready, pads_sent = sem("pad_set"), sem("pads_ready"), sem("pads_sent")
        spare_sent = sem("spare_sent")
        tables_ready = sem("tables_ready")
        w_in = sem("w_in")
        xt_in = [sem(f"xt_in{i}") for i in range(XT)]
        meta_taken = sem("meta_taken")
        x_tr, xT_ready = sem("x_tr"), sem("xT_ready")
        up_done, gelu_done = sem("up_done"), sem("gelu_done")
        h_tr, hT_ready = sem("h_tr"), sem("hT_ready")
        down_done, y_ready = sem("down_done"), sem("y_ready")
        y_turn = sem("y_turn")
        rows_turn = sem("rows_turn")
        ys_sent = [sem(f"ys_sent{i}") for i in range(XT)]
        y_in = [sem(f"y_in{i}") for i in range(B)]
        var2, root2 = sem("var2"), sem("root2")
        out_ready, out_sent = sem("out_ready"), sem("out_sent")

        def x_tile(b, i):
            return x_acc[:, bass.ds(b * QB + i, 1), :].rearrange("p a c -> p (a c)")

        def y_buf(b):
            flat = PT[b // 4][:, :, :, :].rearrange("p h b q -> p (h b q)")
            n = QB * K * C
            return flat[:, (b % 4) * n:(b % 4 + 1) * n].rearrange("p (t c) -> p t c", t=QB)

        block = ctx.enter_context(nc.Block())

        def wait(eng, semaphore, count):
            if not isinstance(count, int) or count > 0:
                eng.wait_ge(semaphore, count)

        def attention_units(eng, emit, peeled=4):
            for n in range(2):
                emit(n, n, n, 0, n == 0, False)
            with eng.Fori(1, PAIRS // 2) as t:
                for n in range(2):
                    emit(2 * t + n, n, None, 0, False, False)
            with eng.Fori(1, B - 1) as b:
                for n in range(peeled):
                    emit(PAIRS * b + n, n % 2, n, b, False, False)
                if peeled < PAIRS:
                    with eng.Fori(peeled // 2, PAIRS // 2) as t:
                        for n in range(2):
                            emit(PAIRS * b + 2 * t + n, n, None, b, False, False)
            for n in range(PAIRS):
                emit(PAIRS * (B - 1) + n, n % 2, n, B - 1, False, n == PAIRS - 1)

        def tiles(eng, emit):
            for n in range(XT):
                emit(n, n, n == 0, False)
            with eng.Fori(1, TILES // XT - 1) as t:
                for n in range(XT):
                    emit(XT * t + n, n, False, False)
            for n in range(XT):
                emit(TILES - XT + n, n, False, n == XT - 1)

        @block.sync
        def _(sp):
            def load_xw(u, p):
                wait(sp, v_proj, u - 1)
                batch, pair = u // PAIRS, u % PAIRS
                sp.dma_start(xs[p][:, :], xT_h[:, bass.ds(batch * T, T)]).then_inc(xw_in[p], 16)
                sp.dma_start(wqkv[p][:, :], wqkv_h[bass.ds(pair, 1), :, :].rearrange("a c n -> c (a n)")).then_inc(xw_in[p], 16)

            def attention_loads(u, p, n, batch, first, last):
                if first:
                    load_xw(0, 0)
                    for dst, src in ((cos_t, cos_h), (sin_t, sin_h), (bo_t, bo_h), (gate_t, gate_h), (ebias_t, ebias_h)):
                        sp.dma_start(dst[:, :], src).then_inc(consts_in, 16)
                    sp.dma_start(x_acc[:, :, :], x_h.rearrange("(t p) c -> p t c", p=P)).then_inc(x_in, 16)
                    sp.dma_start(wup[:, :], wup_h).then_inc(w_in, 16)
                    sp.dma_start(wdown[:, :, :], wdown_h).then_inc(w_in, 16)
                    sp.wait_ge(pad_set, 1)
                    sp.dma_start(xrows[SPARE:SPARE + P, :], pad_row[:, :]).then_inc(spare_sent, 16)
                if not last:
                    load_xw(u + 1, 1 - p)
                wait(sp, y_done, u - 1)
                sp.dma_start(wo[p][:, :], wo_h[bass.ds((u % PAIRS) * P, P), :]).then_inc(wo_in[p], 16)

            attention_units(sp, attention_loads)

            sp.wait_ge(rows_sent, 16 * B * QB * K)
            sp.wait_ge(pads_sent, 16 * E)
            sp.wait_ge(spare_sent, 16)
            sp.wait_ge(tables_ready, 1)

            def tile_loads(t, s, first, last):
                wait(sp, x_tr, t - XT + 1)
                wait(sp, meta_taken, t - XT + 1)
                row = sp.value_load(tile_row[0:1, bass.ds(t, 1)], min_val=0, max_val=SPARE)
                sp.dma_start(xt[s][:, :], xrows[bass.ds(row, P), :]).then_inc(xt_in[s], 16)

            tiles(sp, tile_loads)

            for s in range(XT):
                sp.wait_ge(ys_sent[s], 16 * (TILES // XT))
            y_v = yrows[Y0:Y0 + B * T * K, :].rearrange("(t p k) c -> p t (k c)", p=P, k=K)
            for b in range(B):
                sp.dma_start(y_buf(b), y_v[:, QB * b:QB * b + QB, :]).then_inc(y_in[b], 16)
            out_v = out_h.rearrange("(t p) c -> p t c", p=P)
            for b in range(B):
                sp.wait_ge(out_ready, b + 1)
                sp.dma_start(out_v[:, QB * b:QB * b + QB, :], f_acc[:, QB * b:QB * b + QB, :]).then_inc(out_sent, 16)
            sp.wait_ge(out_sent, 16 * B)

        @block.gpsimd
        def _(pool):
            for p in range(2):
                nc.gpsimd.memset(kM[p][:, :, :], 0.0).then_inc(pool_set, 1)
            nc.gpsimd.memset(ident[:, :], 0.0).then_inc(pool_set, 1)
            nc.gpsimd.memset(causal[:, :], 0.0).then_inc(pool_set, 1)
            nc.gpsimd.iota(order[:, :], pattern=[[-1, E]], base=E, channel_multiplier=0,
                           allow_small_or_imprecise_dtypes=True).then_inc(pool_set, 1)
            nc.gpsimd.memset(pad_row[:, :], 0.0).then_inc(pad_set, 1)
            nc.gpsimd.memset(before_t[:, :], 1.0).then_inc(pool_set, 1)
            nc.gpsimd.memset(ones_t[:, :], 1.0).then_inc(pool_set, 1)
            for dst, pattern, base, step in (
                    (row_id[:, :, :], [[K * P, NT], [1, K]], Y0, K), (pad_id[:, :], [[P, TILES]], 0, 1),
                    (tile_no[:, :], [[1, TILES]], 0, 0), (part_no[:, :], [[0, 1]], 0, 1),
                    (next_row[:, :], [[REGION, E]], 0, 0), (region[:, :], [[REGION, E]], 0, 0)):
                nc.gpsimd.iota(dst, pattern=pattern, base=base, channel_multiplier=step,
                               allow_small_or_imprecise_dtypes=True).then_inc(pool_set, 1)
            pool.wait_ge(pool_set, 13)
            nc.gpsimd.affine_select(out=before_t[:, :], in_=before_t[:, :], compare_op=ALU.is_gt, fill=0.0,
                                    base=0, pattern=[[1, P]], channel_multiplier=-1).then_inc(pool_set, 1)
            nc.gpsimd.affine_select(out=ident[:, :], in_=ident[:, :], compare_op=ALU.not_equal, fill=1.0,
                                    base=0, pattern=[[-1, P]], channel_multiplier=1).then_inc(pool_set, 1)
            nc.gpsimd.affine_select(out=causal[:, T - P:T], in_=causal[:, T - P:T], compare_op=ALU.is_ge, fill=NEG,
                                    base=0, pattern=[[-1, P]], channel_multiplier=1).then_inc(pool_set, 1)
            pool.wait_ge(consts_in, 16 * 5)

            def rotate(u, p):
                pool.wait_ge(q_read, u + 1)
                nc.gpsimd.tensor_tensor(q_rot[:, :], q_rot[:, :], sin_t[:, :], ALU.mult).then_inc(q_mul, 1)
                wait(pool, scored, BLK * (u - 1))
                pool.wait_ge(q_mul, u + 1)
                nc.gpsimd.tensor_tensor(qT[p][:, :], q_cos[:, :], q_rot[:, :], ALU.add).then_inc(q_ready, 1)
                pool.wait_ge(k_read, u + 1)
                nc.gpsimd.tensor_tensor(k_rot[:, :], k_rot[:, :], sin_t[:, :], ALU.mult).then_inc(k_mul, 1)
                pool.wait_ge(k_mul, u + 1)
                for h in range(2):
                    half = slice(D * h, D * h + D)
                    nc.gpsimd.tensor_tensor(kM[p][half, h, :], k_cos[half, :], k_rot[half, :], ALU.add).then_inc(k_ready, 1)

            def send_rows(b, choices):
                for i, k in choices:
                    nc.gpsimd.indirect_dma_start(
                        out=xrows, out_offset=bass.IndirectOffsetOnAxis(ap=slot[:, i, k:k + 1], axis=0),
                        in_=pay[:, i, k, :], in_offset=None).then_inc(rows_sent, 16)

            def rows_ready(b):
                pool.wait_ge(slots_ready, b + 1)
                pool.wait_ge(pay_ready, b + 1)

            def attention(u, p, n, batch, first, last):
                if n == 4 and not (isinstance(batch, int) and batch == 0):
                    rows_ready(batch - 1)
                if n is not None and (n == 0 or n > 4):
                    if not (isinstance(batch, int) and batch == 0):
                        wait(pool, rows_sent, 16 * (QB * K * (batch - 1) + K * max(n - 4, 0)))
                rotate(u, p)
                if n is not None and n >= 4 and not (isinstance(batch, int) and batch == 0):
                    pool.wait_ge(k_ready, 2 * u + 2)
                    pool.sem_inc(rows_turn, 1)
                    send_rows(batch - 1, [(n - 4, 0), (n - 4, 1)])

            attention_units(pool, attention, peeled=PAIRS)
            pool.wait_ge(k_ready, 2 * UNITS)
            rows_ready(B - 1)
            send_rows(B - 1, [(i, k) for i in range(QB) for k in range(K)])
            pool.wait_ge(pads_ready, 1)
            for e in range(E):
                nc.gpsimd.indirect_dma_start(
                    out=xrows, out_offset=bass.IndirectOffsetOnAxis(ap=pad_slot[:, e:e + 1], axis=0),
                    in_=pad_row[:, :], in_offset=None).then_inc(pads_sent, 16)

            def send_y(t, s, first, last):
                pool.wait_ge(y_ready, t + 1)
                pool.sem_inc(y_turn, 1)
                nc.gpsimd.indirect_dma_start(
                    out=yrows, out_offset=bass.IndirectOffsetOnAxis(ap=y_row[s][:, :], axis=0),
                    in_=ys[s][:, :], in_offset=None).then_inc(ys_sent[s], 16)

            tiles(pool, send_y)

        @block.tensor
        def _(pe):
            def project_qk(u, p):
                pe.wait_ge(xw_in[p], 32 * (u // 2 + 1))
                wait(pe, v_ready, u)
                nc.tensor.matmul(QP[:, :], wqkv[p][:, 0:P], xs[p][:, :], start=True, stop=True).then_inc(q_proj, 1)
                wait(pe, k_read, u)
                nc.tensor.matmul(KP[:, :], wqkv[p][:, P:2 * P], xs[p][:, :], start=True, stop=True).then_inc(k_proj, 1)

            def project_v(u, p):
                pe.wait_ge(q_read, u + 1)
                for kb in range(QB):
                    last = nc.tensor.matmul(QP[:, kb * P:kb * P + P], xs[p][:, kb * P:kb * P + P],
                                            wqkv[p][:, 2 * P:3 * P], start=True, stop=True)
                last.then_inc(v_proj, 1)

            def score(u, p, j):
                g, h, qb = BLK * u + j, j // QB, j % QB
                wait(pe, maxed, g - 1)
                nc.tensor.matmul(SB[j % 2][:, 0:(qb + 1) * P], qT[p][:, qb * P:qb * P + P], kM[p][:, h, 0:(qb + 1) * P],
                                 start=True, stop=True).then_inc(scored, 1)

            def transpose(u, p, j):
                g, qb = BLK * u + j, j % QB
                pe.wait_ge(normed, g + 1)
                wait(pe, pt_ready, g - 1)
                for kb in range(qb + 1):
                    last = nc.tensor.transpose(TB[j % 2][:, kb * P:kb * P + P], Pr[j % 4][:, kb * P:kb * P + P], ident[:, :])
                last.then_inc(transposed, 1)

            def attend(u, p):
                pe.wait_ge(pt_ready, BLK * (u + 1))
                pe.wait_ge(v_ready, u + 1)
                wait(pe, o_ready, u)
                for kb in range(QB):
                    for h in range(2):
                        last = nc.tensor.matmul(OB[D * h:D * h + D, kb * P:T], V[p][:, kb, D * h:D * h + D],
                                                PT[p][:, h, kb, kb * P:T], start=(kb == 0), stop=(kb == QB - 1))
                last.then_inc(pv_done, 1)

            def project_out(u, p):
                pe.wait_ge(wo_in[p], 16 * (u // 2 + 1))
                pe.wait_ge(o_ready, u + 1)
                wait(pe, y_added, u)
                for i in range(QB):
                    last = nc.tensor.matmul(YB[:, i * P:i * P + P], OT[p][:, i * P:i * P + P], wo[p][:, :],
                                            start=True, stop=True)
                last.then_inc(y_done, 1)

            def transpose_x1(b, outputs):
                pe.wait_ge(x1_ready, b + 1)
                pe.wait_ge(o_ready, outputs)
                for i in range(QB):
                    last = nc.tensor.transpose(OB[:, i * P:i * P + P], pay[:, i, 0, 0:C], ident[:, :])
                last.then_inc(x1_tr, 1)

            def logits(b):
                pe.wait_ge(x1T_ready, b + 1)
                for i in range(QB):
                    last = nc.tensor.matmul(OB[:, i * E:i * E + E], x1T[:, i * P:i * P + P], gate_t[:, :],
                                            start=True, stop=True)
                last.then_inc(logits_done, 1)

            def rank(b, outputs):
                pe.wait_ge(chosen, b + 1)
                pe.wait_ge(o_ready, outputs)
                flat = cc[:, :, :].rearrange("p n e -> p (n e)")
                nc.tensor.matmul(OB[:, 0:QB * E], before_t[:, :], flat, start=True, stop=True)
                nc.tensor.matmul(OB[:, QB * E:2 * QB * E], ones_t[:, :], flat, start=True, stop=True).then_inc(ranked, 1)

            def attention(u, p, n, batch, first, last):
                route = n is not None and not (isinstance(batch, int) and batch == 0)
                if first:
                    project_qk(0, 0)
                    project_v(0, 0)
                    pe.wait_ge(pool_set, POOL_SET)
                pe.wait_ge(q_ready, u + 1)
                pe.wait_ge(k_ready, 2 * u + 2)
                for j in range(BLK):
                    score(u, p, j)
                    if j >= LAG:
                        transpose(u, p, j - LAG)
                    elif not first:
                        transpose(u - 1, 1 - p, BLK + j - LAG)
                    if j == 2 and not last:
                        project_qk(u + 1, 1 - p)
                    if route and n == 2 and j == 1:
                        logits(batch - 1)
                    if j == 4 and not first:
                        if route and n == 2:
                            pe.wait_ge(gate_sub, batch)
                        if route and n == 3:
                            pe.wait_ge(slots_ready, batch)
                        attend(u - 1, 1 - p)
                    if j == 6 and not last:
                        project_v(u + 1, 1 - p)
                    if route and n == 1 and j == 6:
                        transpose_x1(batch - 1, u)
                    if route and n == 2 and j == 6:
                        rank(batch - 1, u)
                    if j == 7 and not first:
                        project_out(u - 1, 1 - p)

            attention_units(pe, attention)
            u = UNITS - 1
            for j in range(BLK - LAG, BLK):
                transpose(u, 1, j)
            attend(u, 1)
            project_out(u, 1)

            transpose_x1(B - 1, UNITS)
            logits(B - 1)
            pe.wait_ge(gate_sub, B)
            rank(B - 1, UNITS)

            def transpose_x(t, s):
                p = s % 2
                pe.wait_ge(xt_in[s], 16 * (t // XT + 1))
                wait(pe, xT_ready, t - 1)
                nc.tensor.transpose(XB[p][:, 0:P], xt[s][:, 0:C], ident[:, :]).then_inc(x_tr, 1)

            def up(t, s):
                p = s % 2
                e = pe.value_load(tile_expert[0:1, bass.ds(t, 1)], min_val=0, max_val=E - 1)
                pe.wait_ge(xT_ready, t + 1)
                wait(pe, gelu_done, t - 1)
                nc.tensor.matmul(HB[p][:, :], xT[p][:, :], wup[:, bass.ds(e * I, I)], start=True, stop=True).then_inc(up_done, 1)

            def transpose_h(t, s):
                p = s % 2
                pe.wait_ge(gelu_done, t + 1)
                wait(pe, hT_ready, t - 1)
                for ib in range(IB):
                    last = nc.tensor.transpose(GB[p][:, ib * P:ib * P + P], hid[p][:, ib * P:ib * P + P], ident[:, :])
                last.then_inc(h_tr, 1)

            def down(t, s):
                p = s % 2
                e = pe.value_load(tile_expert[0:1, bass.ds(t, 1)], min_val=0, max_val=E - 1)
                pe.wait_ge(hT_ready, t + 1)
                wait(pe, y_ready, t - 1)
                for ib in range(IB):
                    last = nc.tensor.matmul(FB[p][:, 0:C], hT[p][:, ib * P:ib * P + P],
                                            wdown[:, bass.ds(e * IB + ib, 1), :].rearrange("p a c -> p (a c)"),
                                            start=(ib == 0), stop=(ib == IB - 1))
                last.then_inc(down_done, 1)

            def ffn(t, s, first, last):
                if first:
                    pe.wait_ge(tables_ready, 1)
                    pe.wait_ge(w_in, 32)
                    pe.wait_ge(slots_ready, B)
                    pe.wait_ge(y_added, UNITS)
                    pe.wait_ge(v_ready, UNITS)
                    transpose_x(0, 0)
                if not last:
                    transpose_x(t + 1, (s + 1) % XT)
                up(t, s)
                if not (isinstance(t, int) and t < 1):
                    transpose_h(t - 1, (s - 1) % XT)
                if not (isinstance(t, int) and t < 2):
                    down(t - 2, (s - 2) % XT)

            tiles(pe, ffn)
            transpose_h(TILES - 1, XT - 1)
            down(TILES - 2, XT - 2)
            down(TILES - 1, XT - 1)

        @block.scalar
        def _(act):
            def copy_v(u, p):
                act.wait_ge(v_proj, u + 1)
                nc.scalar.activation(V[p][:, :, :], QP[:, :].rearrange("k (b f) -> k b f", b=QB), ACT.Copy).then_inc(v_ready, 1)

            def exp(u, p, j):
                g, qb = BLK * u + j, j % QB
                act.wait_ge(maxed, g + 1)
                wait(act, transposed, g - 3)
                n = (qb + 1) * P
                nc.scalar.activation(Pr[j % 4][:, 0:n], Sm[j % 2][:, 0:n], ACT.Exp, bias=nmax[:, j:j + 1], scale=-1.0,
                                     accum_out=rsum[:, j:j + 1]).then_inc(exped, 1)

            def copy_pt(u, p, j):
                h, qb = j // QB, j % QB
                act.wait_ge(transposed, BLK * u + j + 1)
                nc.scalar.activation(PT[p][:, h, 0:qb + 1, qb * P:qb * P + P],
                                     TB[j % 2][:, 0:(qb + 1) * P].rearrange("k (b q) -> k b q", q=P),
                                     ACT.Copy).then_inc(pt_ready, 1)

            def copy_o(u, p):
                act.wait_ge(pv_done, u + 1)
                nc.scalar.activation(OT[p][:, :], OB[:, :], ACT.Copy).then_inc(o_ready, 1)

            def root(b):
                act.wait_ge(eps_set, 1)
                act.wait_ge(var_ready, b + 1)
                nc.scalar.activation(sd[:, :], mv[:, :, 1], ACT.Sqrt, bias=eps_t[:, 0:1]).then_inc(sd_ready, 1)

            def copy_x1T(b):
                act.wait_ge(x1_tr, b + 1)
                nc.scalar.activation(x1T[:, :], OB[:, :], ACT.Copy).then_inc(x1T_ready, 1)

            def copy_rows(b):
                act.wait_ge(x1_ready, b + 1)
                nc.scalar.activation(pay[:, :, 1, 0:C], pay[:, :, 0, 0:C], ACT.Copy).then_inc(pay_ready, 1)
                nc.scalar.activation(x_acc[:, bass.ds(b * QB, QB), :], pay[:, :, 0, 0:C], ACT.Copy).then_inc(x1_kept, 1)

            def exp_logits(b):
                act.wait_ge(gate_sub, b + 1)
                nc.scalar.activation(wt[:, :, :], lg[:, :, :], ACT.Exp).then_inc(gate_exp, 1)

            def attention(u, p, n, batch, first, last):
                route = n is not None and not (isinstance(batch, int) and batch == 0)
                if first:
                    copy_v(0, 0)
                for j in range(BLK):
                    exp(u, p, j)
                    if j >= LAG:
                        copy_pt(u, p, j - LAG)
                    elif not first:
                        copy_pt(u - 1, 1 - p, BLK + j - LAG)
                    if j == 5 and not first:
                        copy_o(u - 1, 1 - p)
                    if j == 7 and not last:
                        copy_v(u + 1, 1 - p)
                    if route and (n, j) == (1, 1):
                        root(batch - 1)
                    if route and (n, j) == (1, 7):
                        copy_x1T(batch - 1)
                    if route and (n, j) == (2, 3):
                        exp_logits(batch - 1)
                    if route and (n, j) == (2, 5):
                        copy_rows(batch - 1)

            attention_units(act, attention)
            u = UNITS - 1
            for j in range(BLK - LAG, BLK):
                copy_pt(u, 1, j)
            copy_o(u, 1)
            root(B - 1)
            copy_x1T(B - 1)
            exp_logits(B - 1)
            copy_rows(B - 1)

            def copy_xT(t, s):
                act.wait_ge(x_tr, t + 1)
                nc.scalar.activation(xT[s % 2][:, :], XB[s % 2][:, 0:P], ACT.Copy).then_inc(xT_ready, 1)

            def ffn(t, s, first, last):
                if first:
                    copy_xT(0, 0)
                if not last:
                    copy_xT(t + 1, s + 1)
                act.wait_ge(up_done, t + 1)
                wait(act, h_tr, t - 1)
                nc.scalar.activation(hid[s % 2][:, :], HB[s % 2][:, :], ACT.Gelu).then_inc(gelu_done, 1)

            tiles(act, ffn)
            n_root = 0
            for k in range(B + 1):
                for n, b in ((0, k), (1, k - 1)):
                    if 0 <= b < B:
                        n_root += 1
                        act.wait_ge(var2, n_root)
                        nc.scalar.activation(sd2[:, n, QB * b:QB * b + QB], mv2[:, n, QB * b:QB * b + QB, 1],
                                             ACT.Sqrt).then_inc(root2, 1)

        @block.vector
        def _(dve):
            steps = [0]

            def done(ins):
                steps[0] += 1
                ins.then_inc(chain, 1)
                dve.wait_ge(chain, steps[0])

            swap = [i ^ 1 for i in range(32)]

            def rope_q(u):
                dve.wait_ge(q_proj, u + 1)
                wait(dve, q_ready, u)
                nc.vector.tensor_tensor(q_cos[:, :], QP[:, :], cos_t[:, :], ALU.mult)
                nc.vector.stream_shuffle(q_rot[:, :], QP[:, :], swap).then_inc(q_read, 1)

            def rope_k(u):
                dve.wait_ge(k_proj, u + 1)
                wait(dve, k_ready, 2 * u)
                nc.vector.tensor_tensor(k_cos[:, :], KP[:, :], cos_t[:, :], ALU.mult)
                nc.vector.stream_shuffle(k_rot[:, :], KP[:, :], swap).then_inc(k_read, 1)

            def mask_max(u, j):
                n = (j % QB + 1) * P
                nc.vector.tensor_tensor_reduce(out=Sm[j % 2][:, 0:n], in0=SB[j % 2][:, 0:n], in1=causal[:, T - n:T],
                                               scale=-0.125, scalar=HUGE, op0=ALU.add, op1=ALU.min,
                                               accum_out=nmax[:, j:j + 1]).then_inc(maxed, 1)

            def invert(u, j):
                dve.wait_ge(exped, BLK * u + j + 1)
                nc.vector.reciprocal(rinv[:, j:j + 1], rsum[:, j:j + 1]).then_inc(inverted, 1)

            def norm(u, j):
                n = (j % QB + 1) * P
                dve.wait_ge(inverted, BLK * u + j + 1)
                nc.vector.tensor_scalar(Pr[j % 4][:, 0:n], Pr[j % 4][:, 0:n], rinv[:, j:j + 1], None,
                                        ALU.mult).then_inc(normed, 1)

            def add_y(u):
                b = u // PAIRS
                tiles = x_acc[:, bass.ds(b * QB, QB), :]
                dve.wait_ge(y_done, u + 1)
                wait(dve, y_added, u)
                nc.vector.tensor_tensor(tiles, YB[:, :].rearrange("t (b c) -> t b c", b=QB), tiles,
                                        ALU.add).then_inc(y_added, 1)

            def over_e(t):
                return t[:, :].unsqueeze(2).to_broadcast([P, QB, E])

            def over_t(t):
                return t[:, :].unsqueeze(1).to_broadcast([P, QB, E])

            def linked(b, i, ins):
                ins.then_inc(route_step, 1)
                dve.wait_ge(route_step, ROUTE * b + i)

            def read_stats(b):
                for i in range(QB):
                    last = nc.vector.bn_stats(st[:, i, :], x_tile(b, i))
                last.then_inc(stats_done, 1)

            def sum_stats(b):
                for i in range(QB):
                    last = nc.vector.bn_aggr(mv[:, i, :], st[:, i, :])
                last.then_inc(var_ready, 1)

            def norm_x1(b):
                dve.wait_ge(sd_ready, b + 1)
                linked(b, 1, nc.vector.reciprocal(rstd[:, :], sd[:, :]))
                wait(dve, rows_sent, 16 * QB * K * b)
                for i in range(QB):
                    last = nc.vector.tensor_scalar(pay[:, i, 0, 0:C], x_tile(b, i), mv[:, i, 0:1], rstd[:, i:i + 1],
                                                   ALU.subtract, ALU.mult)
                last.then_inc(x1_ready, 1)

            def shift_logits(b):
                dve.wait_ge(logits_done, b + 1)
                linked(b, 2, nc.vector.tensor_tensor(lg[:, :, :], OB[:, 0:QB * E].rearrange("p (n e) -> p n e", e=E),
                                                     over_t(ebias_t), ALU.add))
                linked(b, 3, nc.vector.tensor_reduce(m1[:, :], lg[:, :, :], AX.X, ALU.max))
                nc.vector.tensor_tensor(lg[:, :, :], lg[:, :, :], over_e(m1), ALU.subtract).then_inc(gate_sub, 1)

            def pick(b, i, weights, best, chosen):
                linked(b, i, nc.vector.tensor_reduce(best[:, :], weights[:, :, :], AX.X, ALU.max))
                linked(b, i + 1, nc.vector.tensor_tensor(chosen[:, :, :], weights[:, :, :], over_e(best), ALU.is_equal))
                linked(b, i + 2, nc.vector.tensor_tensor(chosen[:, :, :], chosen[:, :, :], over_t(order), ALU.mult))
                linked(b, i + 3, nc.vector.tensor_reduce(s1[:, :], chosen[:, :, :], AX.X, ALU.max))
                linked(b, i + 4, nc.vector.tensor_tensor(chosen[:, :, :], chosen[:, :, :], over_e(s1), ALU.is_equal))

            def first_choice(b):
                dve.wait_ge(gate_exp, b + 1)
                linked(b, 4, nc.vector.tensor_reduce(s1[:, :], wt[:, :, :], AX.X, ALU.add))
                linked(b, 5, nc.vector.reciprocal(s1[:, :], s1[:, :]))
                linked(b, 6, nc.vector.tensor_tensor(wt[:, :, :], wt[:, :, :], over_e(s1), ALU.mult))
                pick(b, 7, wt, m1, c1)

            def second_choice(b):
                linked(b, 12, nc.vector.scalar_tensor_tensor(out=w2[:, :, :], in0=c1[:, :, :], scalar=-2.0,
                                                             in1=wt[:, :, :], op0=ALU.mult, op1=ALU.add))
                pick(b, 13, w2, m2, c2)
                nc.vector.tensor_tensor(cc[:, :, :], c1[:, :, :], c2[:, :, :], ALU.add).then_inc(chosen, 1)
                linked(b, 18, nc.vector.scalar_tensor_tensor(out=den[:, :], in0=m1[:, :], scalar=GATE_EPS, in1=m2[:, :],
                                                             op0=ALU.add, op1=ALU.add))
                linked(b, 19, nc.vector.reciprocal(den[:, :], den[:, :]))
                for k, best in ((0, m1), (1, m2)):
                    nc.vector.tensor_tensor(pay[:, :, k, C], best[:, :], den[:, :], ALU.mult)

            def find_slots(b):
                dve.wait_ge(ranked, b + 1)
                linked(b, 20, nc.vector.tensor_copy(before_n[:, 0, :], next_row[:, :]))
                for i in range(1, QB):
                    linked(b, 20 + i, nc.vector.tensor_tensor(before_n[:, i, :], before_n[:, i - 1, :],
                                                              OB[:, (QB + i - 1) * E:(QB + i) * E], ALU.add))
                nc.vector.tensor_tensor(next_row[:, :], before_n[:, QB - 1, :], OB[:, (2 * QB - 1) * E:2 * QB * E], ALU.add)
                linked(b, 24, nc.vector.tensor_tensor(slots_f[:, :, :], before_n[:, :, :],
                                                      OB[:, 0:QB * E].rearrange("p (n e) -> p n e", e=E), ALU.add))
                nc.vector.tensor_tensor(c1[:, :, :], c1[:, :, :], slots_f[:, :, :], ALU.mult)
                linked(b, 25, nc.vector.tensor_tensor(c2[:, :, :], c2[:, :, :], slots_f[:, :, :], ALU.mult))
                nc.vector.tensor_reduce(slot_f[:, :, 0], c1[:, :, :], AX.X, ALU.add)
                linked(b, 26, nc.vector.tensor_reduce(slot_f[:, :, 1], c2[:, :, :], AX.X, ALU.add))
                nc.vector.tensor_copy(pay[:, :, :, C + 1], row_id[:, bass.ds(b * QB, QB), :])
                nc.vector.tensor_copy(slot[:, :, :], slot_f[:, :, :]).then_inc(slots_ready, 1)

            def attention(u, p, n, batch, first, last):
                route = n is not None and not (isinstance(batch, int) and batch == 0)
                if first:
                    dve.wait_ge(consts_in, 16 * 5)
                    rope_q(0)
                    rope_k(0)
                    dve.wait_ge(x_in, 16)
                    done(nc.vector.tensor_tensor(x_acc[:, :, :], x_acc[:, :, :],
                                                 bo_t[:, :].unsqueeze(1).to_broadcast([P, NT, C]), ALU.add))
                    nc.vector.memset(eps_t[:, :], LN_EPS).then_inc(eps_set, 1)
                    dve.wait_ge(pool_set, POOL_SET)
                for j in range(BLK):
                    at = (n, j) if route else None
                    if at == (1, 1):
                        dve.wait_ge(y_added, u - 1)
                    if at == (1, 2):
                        dve.wait_ge(stats_done, batch)
                    dve.wait_ge(scored, BLK * u + j + 1)
                    before = (u, j - 2) if j >= 2 else None if first else (u - 1, BLK + j - 2)
                    if before:
                        invert(*before)
                    mask_max(u, j)
                    if before:
                        norm(*before)
                    if j == 3 and not last:
                        rope_q(u + 1)
                    if j == 4 and not last:
                        rope_k(u + 1)
                    if j == 0 and not (isinstance(u, int) and u < 2):
                        add_y(u - 2)
                    for place, step in (((1, 1), read_stats), ((1, 2), sum_stats), ((1, 4), norm_x1), ((2, 2), shift_logits),
                                        ((2, 4), first_choice), ((2, 5), second_choice), ((3, 1), find_slots)):
                        if at == place:
                            step(batch - 1)

            attention_units(dve, attention)
            for j in (BLK - 2, BLK - 1):
                invert(UNITS - 1, j)
                norm(UNITS - 1, j)
            add_y(UNITS - 2)
            add_y(UNITS - 1)
            dve.wait_ge(y_added, UNITS)
            read_stats(B - 1)
            dve.wait_ge(stats_done, B)
            for step in (sum_stats, norm_x1, shift_logits, first_choice, second_choice, find_slots):
                step(B - 1)

            nc.vector.tensor_tensor(pad_f[:, :], next_row[:, :], part_no[:, :].to_broadcast([P, E]), ALU.add)
            done(nc.vector.tensor_tensor(count[:, :], next_row[:, :], region[:, :], ALU.subtract))
            nc.vector.tensor_copy(pad_slot[:, :], pad_f[:, :]).then_inc(pads_ready, 1)
            done(nc.vector.tensor_scalar(tiles_of[:, :], count[:, :], 1.0 / P, (P / 2 - 0.5) / P, ALU.mult, ALU.add))
            done(nc.vector.tensor_scalar(tiles_of[:, :], tiles_of[:, :], MAGIC, None, ALU.add))
            done(nc.vector.tensor_scalar(tiles_of[:, :], tiles_of[:, :], -MAGIC, None, ALU.add))
            done(nc.vector.memset(start[:, :], 0.0))
            for e in range(E):
                done(nc.vector.tensor_tensor(start[:, e + 1:e + 2], start[:, e:e + 1], tiles_of[:, e:e + 1], ALU.add))

            def by_expert(t):
                return t[0:1, 0:E].unsqueeze(1).to_broadcast([1, TILES, E])

            def by_tile(t):
                return t[0:1, :].unsqueeze(2).to_broadcast([1, TILES, E])

            done(nc.vector.tensor_tensor(past[:, :, :], by_tile(tile_no), by_expert(start), ALU.is_ge))
            done(nc.vector.tensor_reduce(exp_f[:, :], past[:, :, :], AX.X, ALU.add))
            done(nc.vector.tensor_scalar(exp_f[:, :], exp_f[:, :], -1.0, None, ALU.add))
            nc.vector.tensor_copy(tile_expert[:, :], exp_f[:, :])
            done(nc.vector.tensor_tensor(past[:, :, :], past[:, :, :], by_expert(start), ALU.mult))
            done(nc.vector.tensor_reduce(row_f[:, :], past[:, :, :], AX.X, ALU.max))
            done(nc.vector.tensor_tensor(row_f[:, :], tile_no[:, :], row_f[:, :], ALU.subtract))
            done(nc.vector.tensor_scalar(row_f[:, :], row_f[:, :], float(P), float(-SPARE), ALU.mult, ALU.add))
            done(nc.vector.scalar_tensor_tensor(out=row_f[:, :], in0=exp_f[:, :], scalar=float(REGION), in1=row_f[:, :],
                                                op0=ALU.mult, op1=ALU.add))
            done(nc.vector.tensor_scalar(ok_f[:, :], tile_no[:, :], start[0:1, E:E + 1], None, ALU.is_lt))
            done(nc.vector.tensor_tensor(row_f[:, :], row_f[:, :], ok_f[:, :], ALU.mult))
            done(nc.vector.tensor_scalar(row_f[:, :], row_f[:, :], float(SPARE), None, ALU.add))
            nc.vector.tensor_copy(tile_row[:, :], row_f[:, :]).then_inc(tables_ready, 1)

            def take_meta(t, s):
                wait(dve, ys_sent[s], 16 * (t // XT))
                dve.wait_ge(xt_in[s], 16 * (t // XT + 1))
                nc.vector.tensor_tensor(y_row[s][:, :], xt[s][:, C + 1:C + 2], pad_id[:, bass.ds(t, 1)], ALU.max)
                nc.vector.tensor_copy(y_weight[s][:, :], xt[s][:, C:C + 1]).then_inc(meta_taken, 1)

            def ffn(t, s, first, last):
                if first:
                    take_meta(0, 0)
                if not last:
                    take_meta(t + 1, (s + 1) % XT)
                if not (isinstance(t, int) and t < 1):
                    copy_hT(t - 1, (s - 1) % XT)
                if not (isinstance(t, int) and t < 2):
                    weight_y(t - 2, (s - 2) % XT)

            def copy_hT(t, s):
                dve.wait_ge(h_tr, t + 1)
                nc.vector.tensor_copy(hT[s % 2][:, :], GB[s % 2][:, :]).then_inc(hT_ready, 1)

            def weight_y(t, s):
                dve.wait_ge(meta_taken, t + 1)
                dve.wait_ge(down_done, t + 1)
                nc.vector.tensor_scalar(ys[s][:, :], FB[s % 2][:, 0:C], y_weight[s][:, :], None, ALU.mult).then_inc(y_ready, 1)

            tiles(dve, ffn)
            copy_hT(TILES - 1, XT - 1)
            weight_y(TILES - 2, XT - 2)
            weight_y(TILES - 1, XT - 1)

            def stats2(n, b):
                for i in range(QB * b, QB * b + QB):
                    last = nc.vector.bn_stats(st2[:, i, :], f_acc[:, i, :])
                done(last)
                for i in range(QB * b, QB * b + QB):
                    last = nc.vector.bn_aggr(mv2[:, n, i, :], st2[:, i, :])
                done(last)
                nc.vector.tensor_scalar(mv2[:, n, QB * b:QB * b + QB, 1], mv2[:, n, QB * b:QB * b + QB, 1], LN_EPS, None,
                                        ALU.add).then_inc(var2, 1)

            def norm2(n, b, roots):
                dve.wait_ge(root2, roots)
                done(nc.vector.reciprocal(rstd2[:, n, QB * b:QB * b + QB], sd2[:, n, QB * b:QB * b + QB]))
                for i in range(QB * b, QB * b + QB):
                    last = nc.vector.tensor_scalar(f_acc[:, i, :], f_acc[:, i, :], mv2[:, n, i, 0:1], rstd2[:, n, i:i + 1],
                                                   ALU.subtract, ALU.mult)
                return last

            dve.wait_ge(x1_kept, B)
            for k in range(B + 2):
                if k < B:
                    y = y_buf(k)
                    dve.wait_ge(y_in[k], 16)
                    done(nc.vector.tensor_tensor(f_acc[:, QB * k:QB * k + QB, :], y[:, :, 0:C], y[:, :, C:K * C], ALU.add))
                    stats2(0, k)
                if 1 <= k <= B:
                    b = k - 1
                    done(norm2(0, b, 1 if b == 0 else 2 * b))
                    done(nc.vector.scalar_tensor_tensor(
                        out=f_acc[:, QB * b:QB * b + QB, :], in0=x_acc[:, QB * b:QB * b + QB, :], scalar=2.0,
                        in1=f_acc[:, QB * b:QB * b + QB, :], op0=ALU.mult, op1=ALU.add))
                    stats2(1, b)
                if k >= 2:
                    b = k - 2
                    norm2(1, b, min(2 * b + 3, 2 * B)).then_inc(out_ready, 1)


def rope_tables():
    import numpy as np
    inv_freq = (np.float32(1.0) / np.float32(10000.0) ** (np.arange(0, D, 2, dtype=np.float32) / np.float32(D))).astype(np.float32)
    ang = (np.arange(T, dtype=np.float32)[None, :] * inv_freq[:, None]).astype(np.float32)
    sign = np.array([-1.0, 1.0], np.float32)[:, None]
    cos = np.tile(np.repeat(np.cos(ang), 2, axis=0), (2, 1))
    sin = np.tile((np.sin(ang)[:, None, :] * sign).reshape(D, T), (2, 1))
    return np.ascontiguousarray(cos, np.float32), np.ascontiguousarray(sin, np.float32)


def kernel(**inputs):
    import numpy as np
    import concourse.bacc as bacc
    from concourse.bass_utils import run_bass_kernel_spmd

    a = {k.replace("L0_", ""): np.asarray(v) for k, v in inputs.items()}
    cos, sin = rope_tables()
    x = a["attn_x"].reshape(B * T, C)
    qkv = [a[f"attn_W{n}"].reshape(C, PAIRS, P).transpose(1, 0, 2) for n in "qkv"]
    arrays = {
        "xT": x.T,
        "x": x,
        "wqkv": np.concatenate(qkv, axis=2),
        "wo": a["attn_Wo"],
        "bo": np.broadcast_to(a["attn_bo"], (P, C)),
        "cos": cos,
        "sin": sin,
        "gate": a["ffn_gate_w"].T,
        "ebias": np.broadcast_to(a["ffn_expert_bias"], (P, E)),
        "wup": a["ffn_w_up"].reshape(E * I, C).T,
        "wdown": a["ffn_w_down"].reshape(E, C, IB, P).transpose(3, 0, 2, 1).reshape(P, E * IB, C),
    }
    arrays = {f"in_{k}": np.ascontiguousarray(v) for k, v in arrays.items()}
    nc = bacc.Bacc("TRN2", target_bir_lowering=False, num_devices=1)
    args = [nc.dram_tensor(k, v.shape, mybir.dt.from_np(v.dtype), kind="ExternalInput").ap() for k, v in arrays.items()]
    args.append(nc.dram_tensor("xrows", (SPARE + P, ROW), F32, kind="Internal").ap())
    args.append(nc.dram_tensor("yrows", (Y0 + B * T * K, C), F32, kind="Internal").ap())
    out = nc.dram_tensor("out_0", (B * T, C), F32, kind="ExternalOutput").ap()
    build_block(nc, *args, out)
    r = run_bass_kernel_spmd(nc, [arrays], core_ids=[0])
    return r.results[0]["out_0"].reshape(B, T, C)
```

```python
import concourse.bass as bass
from concourse import mybir
from contextlib import ExitStack

F32 = mybir.dt.float32
F32R = mybir.dt.float32r
ALU = mybir.AluOpType
ACT = mybir.ActivationFunctionType
AX = mybir.AxisListType

P = 128
B, T, C = 8, 512, 128
D = 64
HEADS = 16
PAIRS = HEADS // 2
E, I = 8, 512
QB = T // P
NT = B * QB
IB = I // P
UNITS = B * PAIRS
BLK = 2 * QB
ORDER = [(0, 3), (0, 1), (1, 3), (0, 2), (1, 2), (1, 1), (0, 0), (1, 0)]
ROOT_AT = (1, 7)
LAG = 4
K = 2
TILES = (B * T * K + E * (P - 1)) // P + 1
TILES += -TILES % 4
REGION = B * T + P
SPARE = E * REGION
Y0 = TILES * P
ROW = C + 2
XT = 4
QJ, KJ, AJ, VJ, YJ = 1, 3, 4, 5, 7
LN_EPS = 1e-5
VAR, X1, LOGITS_READ, SHIFTED, CHOSEN, RANKS_READ, SLOTS, ROUTE = 3, 5, 6, 8, 23, 26, 34, 34
POOL_SET = 15
MAGIC = 1.5 * 2.0 ** 23
I32 = mybir.dt.int32
GATE_EPS = 1e-6
NEG = -3.0e38
HUGE = 3.0e38


def build_block(nc, xT_h, x_h, wqk_h, wv_h, wo_h, bo_h, cos_h, sin_h, gate_h, ebias_h, wup_h, wdown_h, xrows, yrows, out_h):
    ctx = ExitStack()
    with ctx:
        def sb(name, shape, dtype=F32):
            return ctx.enter_context(nc.sbuf_tensor(name, shape, dtype))

        def ps(name):
            return ctx.enter_context(nc.psum_tensor(name, [P, 512], F32))

        def sem(name):
            return ctx.enter_context(nc.semaphore(name))

        ident = sb("ident", [P, P])
        causal = sb("causal", [P, T])
        cos_t = sb("cos_t", [P, T])
        sin_t = sb("sin_t", [P, T])
        bo_t = sb("bo_t", [P, C])
        gate_t = sb("gate_t", [P, E])
        ebias_t = sb("ebias_t", [P, E])
        order = sb("order", [P, E])
        before_t = sb("before_t", [P, P])
        ones_t = sb("ones_t", [P, P])
        row_id = sb("row_id", [P, NT, K])
        pad_id = sb("pad_id", [P, TILES])
        tile_no = sb("tile_no", [1, TILES])
        eps_t = sb("eps_t", [P, 1])
        warm = sb("warm", [P, 1])
        region = sb("region", [P, E])
        pad_rows = sb("pad_rows", [P, ROW])
        x_acc = sb("x_acc", [P, NT, C])
        x_next = sb("x_next", [P, T])
        x_cur = sb("x_cur", [P, T])
        x_hi, x_lo = sb("x_hi", [P, T], F32R), sb("x_lo", [P, T], F32R)
        wqk = sb("wqk", [P, PAIRS // 2, 2, 4 * P], F32R)
        wv = sb("wv", [P, PAIRS, P])
        wo = [sb(f"wo{i}", [P, C]) for i in range(2)]
        qT = [sb(f"qT{i}", [P, T]) for i in range(2)]
        kM = [sb(f"kM{i}", [P, 2, T]) for i in range(2)]
        V = [sb(f"V{i}", [P, QB, P]) for i in range(2)]
        PT = [sb(f"PT{i}", [P, 2, QB, T]) for i in range(2)]
        OT = [sb(f"OT{i}", [P, T]) for i in range(2)]
        Sm = [sb(f"Sm{i}", [P, T]) for i in range(4)]
        Pr_all = sb("Pr_all", [P, BLK, T])
        Pr = [Pr_all[:, i, :] for i in range(BLK)]
        q_cos, q_rot, k_cos, k_rot = (sb(n, [P, T]) for n in ("q_cos", "q_rot", "k_cos", "k_rot"))
        nmax = sb("nmax", [P, BLK])
        rsum = sb("rsum", [P, BLK])
        rinv = sb("rinv", [P, BLK])
        st = sb("st", [P, QB, 6])
        mv = sb("mv", [P, QB, 2])
        sd = sb("sd", [P, QB])
        rstd = sb("rstd", [P, QB])
        x1T = sb("x1T", [P, T])
        ranks = sb("ranks", [P, 2 * QB, E])
        lg, wt, w2, c1, c2, cc, slots_f = (sb(n, [P, QB, E]) for n in ("lg", "wt", "w2", "c1", "c2", "cc", "slots_f"))
        m1, m2, s1, den = (sb(n, [P, QB]) for n in ("m1", "m2", "s1", "den"))
        before_n = sb("before_n", [P, QB, E])
        next_row = sb("next_row", [P, E])
        slot_f = sb("slot_f", [P, QB, K])
        slot = sb("slot", [P, QB, K], I32)
        pay = sb("pay", [P, QB, K, ROW])
        count = sb("count", [P, E])
        tiles_of = sb("tiles_of", [P, E])
        sums = [sb(f"sums{i}", [P, E]) for i in range(2)]
        start = sb("start", [P, E + 1])
        past = sb("past", [1, TILES, E])
        exp_f, row_f, ok_f = (sb(n, [1, TILES]) for n in ("exp_f", "row_f", "ok_f"))
        tile_expert = sb("tile_expert", [1, TILES], I32)
        tile_row = sb("tile_row", [1, TILES], I32)
        pad_at = sb("pad_at", [1, E], I32)
        wup = sb("wup", [P, E * I])
        wdown = sb("wdown", [P, E * IB, C])
        xt = [sb(f"xt{i}", [P, ROW]) for i in range(XT)]
        xT = [sb(f"xT{i}", [P, P]) for i in range(2)]
        w_tile = [sb(f"w_tile{i}", [P, I]) for i in range(2)]
        hT = [sb(f"hT{i}", [P, I]) for i in range(2)]
        w_stage = [w_tile[0], w_tile[1], hT[0], hT[1]]
        ys = [sb(f"ys{i}", [P, C]) for i in range(XT)]
        y_row = [sb(f"y_row{i}", [P, 1], I32) for i in range(XT)]
        y_weight = [sb(f"y_weight{i}", [P, 1]) for i in range(XT)]
        f_acc = Pr_all[:, :, :].rearrange("p b (n c) -> p (b n) c", c=C)
        st2 = sb("st2", [P, 2, NT, 6])
        mv2 = sb("mv2", [P, 2, NT, 2])
        sd2 = sb("sd2", [P, 2, NT])
        rstd2 = sb("rstd2", [P, 2, NT])
        shift2 = sb("shift2", [P, 2, NT])

        SB = [ps(f"SB{i}") for i in range(4)]
        TB = [ps("TB0"), ps("TB1")]
        AB = ps("AB")
        OB = ps("OB")
        XB, HB, FB = [AB, SB[3]], SB[0:2], [OB, SB[2]]

        consts_in = sem("consts_in")
        x_in = sem("x_in")
        x0_in, wv_in, x_next_in = sem("x0_in"), sem("wv_in"), sem("x_next_in")
        wqk_in = [sem(f"wqk_in{i}") for i in range(PAIRS // 2)]
        w_high, w_split = sem("w_high"), sem("w_split")
        x_high, x_split, x_moved = sem("x_high"), sem("x_split"), sem("x_moved")
        wo_in = [sem("wo_in0"), sem("wo_in1")]
        pool_set = sem("pool_set")
        q_proj, k_proj, v_proj = sem("q_proj"), sem("k_proj"), sem("v_proj")
        q_read, k_read = sem("q_read"), sem("k_read")
        q_mul, k_mul = sem("q_mul"), sem("k_mul")
        q_ready, k_ready, v_ready = sem("q_ready"), sem("k_ready"), sem("v_ready")
        scored = sem("scored")
        maxed = sem("maxed")
        exped = sem("exped")
        inverted = sem("inverted")
        normed = sem("normed")
        transposed = sem("transposed")
        pt_ready = sem("pt_ready")
        pv_done = sem("pv_done")
        o_ready = sem("o_ready")
        y_done = sem("y_done")
        y_added = sem("y_added")
        x_set = sem("x_set")
        chain = sem("chain")
        eps_set = sem("eps_set")
        routed = sem("routed")
        x1_kept = sem("x1_kept")
        stats_turn = sem("stats_turn")
        sd_ready = sem("sd_ready")
        x1_tr, x1T_ready = sem("x1_tr"), sem("x1T_ready")
        pay_ready = sem("pay_ready")
        logits_done = sem("logits_done")
        gate_exp = sem("gate_exp")
        ranked = sem("ranked")
        rows_sent = sem("rows_sent")
        pad_set, pads_ready, pads_sent = sem("pad_set"), sem("pads_ready"), sem("pads_sent")
        spare_sent = sem("spare_sent")
        tables_ready = sem("tables_ready")
        w_in = sem("w_in")
        xt_in = [sem(f"xt_in{i}") for i in range(XT)]
        meta_taken = sem("meta_taken")
        x_tr, xT_ready = sem("x_tr"), sem("xT_ready")
        up_done, gelu_done = sem("up_done"), sem("gelu_done")
        w_ready = sem("w_ready")
        down_done, y_ready = sem("down_done"), sem("y_ready")
        y_turn = sem("y_turn")
        rows_turn = sem("rows_turn")
        ys_sent = [sem(f"ys_sent{i}") for i in range(XT)]
        y_in = [sem(f"y_in{i}") for i in range(B)]
        var2, root2 = sem("var2"), sem("root2")
        root_inverted = sem("root_inverted")
        y_summed, stats_in, factors_ready = sem("y_summed"), sem("stats_in"), sem("factors_ready")
        normed2, x1_twice = sem("normed2"), sem("x1_twice")
        last_normed = sem("last_normed")
        out_sent = sem("out_sent")

        def x_tile(b, i):
            return x_acc[:, bass.ds(b * QB + i, 1), :].rearrange("p a c -> p (a c)")

        def y_buf(b):
            flat = PT[b // 4][:, :, :, :].rearrange("p h b q -> p (h b q)")
            n = QB * K * C
            return flat[:, (b % 4) * n:(b % 4 + 1) * n].rearrange("p (t c) -> p t c", t=QB)

        block = ctx.enter_context(nc.Block())

        def wait(eng, semaphore, count):
            if not isinstance(count, int) or count > 0:
                eng.wait_ge(semaphore, count)

        def last_batch(batch):
            return isinstance(batch, int) and batch == B - 1

        def attention_units(eng, emit, peeled=PAIRS):
            for n in range(PAIRS):
                emit(n, n % 2, n, 0, n == 0, False)
            with eng.Fori(1, B - 1) as b:
                for n in range(peeled):
                    emit(PAIRS * b + n, n % 2, n, b, False, False)
                if peeled < PAIRS:
                    with eng.Fori(peeled // 2, PAIRS // 2) as t:
                        for n in range(2):
                            emit(PAIRS * b + 2 * t + n, n, None, b, False, False)
            for n in range(PAIRS):
                emit(PAIRS * (B - 1) + n, n % 2, n, B - 1, False, n == PAIRS - 1)

        def tiles(eng, emit):
            for n in range(XT):
                emit(n, n, n == 0, False)
            with eng.Fori(1, TILES // XT - 1) as t:
                for n in range(XT):
                    emit(XT * t + n, n, False, False)
            for n in range(XT):
                emit(TILES - XT + n, n, False, n == XT - 1)

        def norm_order(delay):
            pairs = [((0, k), (1, k - 1)) if delay == 1 else ((1, k - 2), (0, k)) for k in range(B + 2)]
            return [(n, b) for pair in pairs for n, b in pair if 0 <= b < B]

        def gathered(n, b):
            return norm_order(1).index((n, b)) + 1

        def scaled(n, b):
            return norm_order(2).index((n, b)) + 1

        @block.sync
        def _(sp):
            def attention_loads(u, p, n, batch, first, last):
                if first:
                    sp.dma_start(x_cur[:, :], xT_h[:, 0:T]).then_inc(x0_in, 16)
                    for i in range(PAIRS // 2):
                        sp.dma_start(w_stage[i][:, :], wqk_h[:, i * 4 * P:(i + 1) * 4 * P]).then_inc(wqk_in[i], 16)
                        if i == 0:
                            for dst, src in ((cos_t, cos_h), (sin_t, sin_h), (bo_t, bo_h), (gate_t, gate_h), (ebias_t, ebias_h)):
                                sp.dma_start(dst[:, :], src).then_inc(consts_in, 16)
                            sp.dma_start(wv[:, :, :], wv_h.rearrange("c (p n) -> c p n", p=PAIRS)).then_inc(wv_in, 16)
                if n == 0 and not last_batch(batch):
                    wait(sp, x_moved, batch)
                    wait(sp, x_split, batch)
                    sp.dma_start(x_next[:, :], xT_h[:, bass.ds(batch * T + T, T)]).then_inc(x_next_in, 16)
                wait(sp, y_done, u - 1)
                sp.dma_start(wo[p][:, :], wo_h[bass.ds((u % PAIRS) * P, P), :]).then_inc(wo_in[p], 16)
                if first:
                    sp.dma_start(x_acc[:, :, :], x_h.rearrange("(t p) c -> p t c", p=P)).then_inc(x_in, 16)
                if isinstance(u, int) and u == 1:
                    sp.dma_start(wup[:, :], wup_h).then_inc(w_in, 16)
                    sp.dma_start(wdown[:, :, :], wdown_h).then_inc(w_in, 16)
                    sp.wait_ge(pad_set, 1)
                    sp.dma_start(xrows[SPARE:SPARE + P, :], pad_rows[:, :]).then_inc(spare_sent, 16)

            attention_units(sp, attention_loads, peeled=2)

            sp.wait_ge(pads_ready, 1)
            for e in range(E):
                row = sp.value_load(pad_at[0:1, e:e + 1], min_val=0, max_val=SPARE)
                sp.dma_start(xrows[bass.ds(row, P), :], pad_rows[:, :]).then_inc(pads_sent, 16)
            sp.wait_ge(rows_sent, 16 * B * QB * K)
            sp.wait_ge(pads_sent, 16 * E)
            sp.wait_ge(spare_sent, 16)
            sp.wait_ge(tables_ready, 1)

            def tile_loads(t, s, first, last):
                wait(sp, x_tr, t - XT + 1)
                wait(sp, meta_taken, t - XT + 1)
                row = sp.value_load(tile_row[0:1, bass.ds(t, 1)], min_val=0, max_val=SPARE)
                sp.dma_start(xt[s][:, :], xrows[bass.ds(row, P), :]).then_inc(xt_in[s], 16)

            tiles(sp, tile_loads)

            for s in range(XT):
                sp.wait_ge(ys_sent[s], 16 * (TILES // XT))
            y_v = yrows[Y0:Y0 + B * T * K, :].rearrange("(t p k) c -> p t (k c)", p=P, k=K)
            for b in range(B):
                sp.dma_start(y_buf(b), y_v[:, QB * b:QB * b + QB, :]).then_inc(y_in[b], 16)
            out_v = out_h.rearrange("(t p) c -> p t c", p=P)
            for b in range(B):
                sp.wait_ge(normed2, scaled(1, b))
                sp.wait_ge(last_normed, b + 1)
                sp.dma_start(out_v[:, QB * b:QB * b + QB, :], f_acc[:, QB * b:QB * b + QB, :]).then_inc(out_sent, 16)
            sp.wait_ge(out_sent, 16 * B)

        @block.gpsimd
        def _(pool):
            for p in range(2):
                nc.gpsimd.memset(kM[p][:, :, :], 0.0).then_inc(pool_set, 1)
            nc.gpsimd.memset(ident[:, :], 0.0).then_inc(pool_set, 1)
            nc.gpsimd.memset(causal[:, :], 0.0).then_inc(pool_set, 1)
            nc.gpsimd.iota(order[:, :], pattern=[[-1, E]], base=E, channel_multiplier=0,
                           allow_small_or_imprecise_dtypes=True).then_inc(pool_set, 1)
            nc.gpsimd.memset(pad_rows[:, :], 0.0).then_inc(pad_set, 1)
            nc.gpsimd.memset(before_t[:, :], 1.0).then_inc(pool_set, 1)
            nc.gpsimd.memset(ones_t[:, :], 1.0).then_inc(pool_set, 1)
            for dst, pattern, base, step in (
                    (row_id[:, :, :], [[K * P, NT], [1, K]], Y0, K), (pad_id[:, :], [[P, TILES]], 0, 1),
                    (tile_no[:, :], [[1, TILES]], 0, 0),
                    (next_row[:, :], [[REGION, E]], 0, 0), (region[:, :], [[REGION, E]], 0, 0)):
                nc.gpsimd.iota(dst, pattern=pattern, base=base, channel_multiplier=step,
                               allow_small_or_imprecise_dtypes=True).then_inc(pool_set, 1)
            pool.wait_ge(pool_set, 12)
            nc.gpsimd.affine_select(out=before_t[:, :], in_=before_t[:, :], compare_op=ALU.is_gt, fill=0.0,
                                    base=0, pattern=[[1, P]], channel_multiplier=-1).then_inc(pool_set, 1)
            nc.gpsimd.affine_select(out=ident[:, :], in_=ident[:, :], compare_op=ALU.not_equal, fill=1.0,
                                    base=0, pattern=[[-1, P]], channel_multiplier=1).then_inc(pool_set, 1)
            nc.gpsimd.affine_select(out=causal[:, T - P:T], in_=causal[:, T - P:T], compare_op=ALU.is_ge, fill=NEG,
                                    base=0, pattern=[[-1, P]], channel_multiplier=1).then_inc(pool_set, 1)
            pool.wait_ge(consts_in, 16 * 5)

            def rotate(u, p):
                pool.wait_ge(q_read, u + 1)
                nc.gpsimd.tensor_tensor(q_rot[:, :], q_rot[:, :], sin_t[:, :], ALU.mult).then_inc(q_mul, 1)
                wait(pool, scored, BLK * (u - 1))
                pool.wait_ge(q_mul, u + 1)
                nc.gpsimd.tensor_tensor(qT[p][:, :], q_cos[:, :], q_rot[:, :], ALU.add).then_inc(q_ready, 1)
                if isinstance(u, int) and u == 0:
                    return
                pool.wait_ge(k_read, u + 1)
                nc.gpsimd.tensor_tensor(k_rot[:, :], k_rot[:, :], sin_t[:, :], ALU.mult).then_inc(k_mul, 1)
                pool.wait_ge(k_mul, u + 1)
                for h in range(2):
                    half = slice(D * h, D * h + D)
                    nc.gpsimd.tensor_tensor(kM[p][half, h, :], k_cos[half, :], k_rot[half, :], ALU.add).then_inc(k_ready, 1)

            def split_weights(i):
                pool.wait_ge(wqk_in[i], 16)
                nc.gpsimd.tensor_copy(wqk[:, i, 0, :], w_stage[i][:, :]).then_inc(w_high, 1)
                pool.wait_ge(w_high, i + 1)
                nc.gpsimd.tensor_tensor(wqk[:, i, 1, :], w_stage[i][:, :], wqk[:, i, 0, :], ALU.subtract).then_inc(w_split, 1)

            def send_rows(b, choices):
                for i, k in choices:
                    nc.gpsimd.indirect_dma_start(
                        out=xrows, out_offset=bass.IndirectOffsetOnAxis(ap=slot[:, i, k:k + 1], axis=0),
                        in_=pay[:, i, k, :], in_offset=None).then_inc(rows_sent, 16)

            def rows_ready(b):
                pool.wait_ge(routed, ROUTE * b + SLOTS)
                pool.wait_ge(pay_ready, b + 1)

            all_rows = [(i, k) for i in range(QB) for k in range(K)]
            sends = {6: all_rows[0:4], 7: all_rows[4:8]}

            def attention(u, p, n, batch, first, last):
                route = n is not None and not (isinstance(batch, int) and batch == 0)
                if route and n in (0, 7):
                    sent = {0: 0, 7: 4}[n]
                    wait(pool, rows_sent, 16 * (QB * K * (batch - 1) + sent))
                rotate(u, p)
                if isinstance(u, int) and 2 <= u < 2 + PAIRS // 2:
                    pool.wait_ge(k_ready, 2 * u + 2)
                    split_weights(u - 2)
                if route and n in sends:
                    pool.wait_ge(k_ready, 2 * u + 2)
                    if n == min(sends):
                        rows_ready(batch - 1)
                    pool.sem_inc(rows_turn, 1)
                    send_rows(batch - 1, sends[n])

            attention_units(pool, attention)
            pool.wait_ge(k_ready, 2 * UNITS)
            rows_ready(B - 1)
            send_rows(B - 1, all_rows)
            def send_y(t, s, first, last):
                pool.wait_ge(y_ready, t + 1)
                pool.sem_inc(y_turn, 1)
                nc.gpsimd.indirect_dma_start(
                    out=yrows, out_offset=bass.IndirectOffsetOnAxis(ap=y_row[s][:, :], axis=0),
                    in_=ys[s][:, :], in_offset=None).then_inc(ys_sent[s], 16)

            tiles(pool, send_y)

            def sum_choices(b):
                y = y_buf(b)
                pool.wait_ge(y_in[b], 16)
                nc.gpsimd.tensor_tensor(f_acc[:, QB * b:QB * b + QB, :], y[:, :, 0:C], y[:, :, C:K * C],
                                        ALU.add).then_inc(y_summed, 1)

            def norm_last(b):
                i = QB * b + QB - 1
                pool.wait_ge(factors_ready, scaled(1, b))
                nc.gpsimd.tensor_scalar(f_acc[:, i, :], f_acc[:, i, :], mv2[:, 1, i, 0:1], rstd2[:, 1, i:i + 1],
                                        ALU.subtract, ALU.mult).then_inc(last_normed, 1)

            for k in range(3):
                sum_choices(k)
            for k in range(2, B + 2):
                if k + 1 < B:
                    sum_choices(k + 1)
                norm_last(k - 2)

        @block.tensor
        def _(pe):
            def project(bank, n, which, batch):
                at = (n % 2) * 2 * P + which * P
                if isinstance(batch, int) and batch == 0:
                    return nc.tensor.matmul(bank[:, :], w_stage[n // 2][:, at:at + P], x_cur[:, :], start=True, stop=True)
                high, low = (wqk[:, n // 2, i, at:at + P] for i in range(2))
                nc.tensor.matmul(bank[:, :], high, x_hi[:, :], start=True, stop=False)
                nc.tensor.matmul(bank[:, :], low, x_hi[:, :], start=False, stop=False)
                return nc.tensor.matmul(bank[:, :], high, x_lo[:, :], start=False, stop=True)

            def project_q(u, n, batch):
                if isinstance(batch, int) and batch == 0:
                    pe.wait_ge(wqk_in[n // 2], 16)
                    pe.wait_ge(x0_in, 16)
                elif n == 0:
                    pe.wait_ge(w_split, PAIRS // 2)
                    pe.wait_ge(x_split, batch)
                wait(pe, v_ready, u)
                project(AB, n, 0, batch).then_inc(q_proj, 1)

            def project_k(u, n, batch, bank=AB):
                if bank is AB:
                    pe.wait_ge(q_read, u + 1)
                project(bank, n, 1, batch).then_inc(k_proj, 1)

            def project_v(u, n, batch, bank=AB):
                if isinstance(u, int) and u == 0:
                    pe.wait_ge(wv_in, 16)
                if bank is AB:
                    pe.wait_ge(k_read, u + 1)
                if n == 0:
                    wait(pe, x_moved, batch)
                for kb in range(QB):
                    last = nc.tensor.matmul(bank[:, kb * P:kb * P + P], x_cur[:, kb * P:kb * P + P],
                                            wv[:, n, :], start=True, stop=True)
                last.then_inc(v_proj, 1)

            def score(u, p, j):
                g, (h, qb) = BLK * u + j, ORDER[j]
                wait(pe, maxed, g - 3)
                nc.tensor.matmul(SB[j % 4][:, 0:(qb + 1) * P], qT[p][:, qb * P:qb * P + P], kM[p][:, h, 0:(qb + 1) * P],
                                 start=True, stop=True).then_inc(scored, 1)

            def transpose(u, p, j):
                g, qb = BLK * u + j, ORDER[j][1]
                pe.wait_ge(normed, g + 1)
                wait(pe, pt_ready, g - 1)
                for kb in range(qb + 1):
                    last = nc.tensor.transpose(TB[j % 2][:, kb * P:kb * P + P], Pr[j][:, kb * P:kb * P + P], ident[:, :])
                last.then_inc(transposed, 1)

            def attend(u, p, blocks):
                if blocks[0] == 0:
                    pe.wait_ge(pt_ready, BLK * (u + 1))
                    pe.wait_ge(v_ready, u + 1)
                    wait(pe, y_added, u)
                for kb in blocks:
                    for h in range(2):
                        last = nc.tensor.matmul(OB[D * h:D * h + D, kb * P:T], V[p][:, kb, D * h:D * h + D],
                                                PT[p][:, h, kb, kb * P:T], start=(kb == 0), stop=(kb == QB - 1))
                if blocks[-1] == QB - 1:
                    last.then_inc(pv_done, 1)

            def project_out(u, p):
                pe.wait_ge(wo_in[p], 16 * (u // 2 + 1))
                pe.wait_ge(o_ready, u + 1)
                for i in range(QB):
                    last = nc.tensor.matmul(OB[:, i * P:i * P + P], OT[p][:, i * P:i * P + P], wo[p][:, :],
                                            start=True, stop=True)
                last.then_inc(y_done, 1)

            def transpose_x1(b, outputs):
                pe.wait_ge(routed, ROUTE * b + X1)
                pe.wait_ge(y_added, outputs)
                for i in range(QB):
                    last = nc.tensor.transpose(OB[:, i * P:i * P + P], pay[:, i, 0, 0:C], ident[:, :])
                last.then_inc(x1_tr, 1)

            def logits(b):
                pe.wait_ge(x1T_ready, b + 1)
                for i in range(QB):
                    last = nc.tensor.matmul(OB[:, i * E:i * E + E], x1T[:, i * P:i * P + P], gate_t[:, :],
                                            start=True, stop=True)
                last.then_inc(logits_done, 1)

            def rank(b, outputs):
                pe.wait_ge(routed, ROUTE * b + CHOSEN)
                pe.wait_ge(y_added, outputs)
                flat = cc[:, :, :].rearrange("p n e -> p (n e)")
                nc.tensor.matmul(OB[:, 0:QB * E], before_t[:, :], flat, start=True, stop=True)
                nc.tensor.matmul(OB[:, QB * E:2 * QB * E], ones_t[:, :], flat, start=True, stop=True).then_inc(ranked, 1)

            def attention(u, p, n, batch, first, last):
                route = n is not None and not (isinstance(batch, int) and batch == 0)
                if first:
                    project_q(0, 0, 0)
                    project_k(0, 0, 0, SB[2])
                    project_v(0, 0, 0, SB[3])
                    pe.wait_ge(pool_set, POOL_SET)
                following = ((n + 1) % PAIRS, batch + 1 if n == PAIRS - 1 else batch)
                pe.wait_ge(q_ready, u + 1)
                pe.wait_ge(k_ready, 2 * u + 2)
                for j in range(BLK):
                    if first and j == 3:
                        pe.wait_ge(v_ready, 1)
                    score(u, p, j)
                    if j >= LAG:
                        transpose(u, p, j - LAG)
                    elif not first:
                        transpose(u - 1, 1 - p, BLK + j - LAG)
                    if j == QJ and not last:
                        project_q(u + 1, *following)
                    if j == KJ and not last:
                        project_k(u + 1, *following)
                    if route and (n, j) == (3, 1):
                        transpose_x1(batch - 1, u - 1)
                    if route and (n, j) == (3, 3):
                        logits(batch - 1)
                    if route and (n, j) == (5, 1):
                        rank(batch - 1, u - 1)
                    if j == AJ and not first:
                        if route and n == 3:
                            pe.wait_ge(routed, ROUTE * (batch - 1) + LOGITS_READ)
                        if route and n == 5:
                            pe.wait_ge(routed, ROUTE * (batch - 1) + RANKS_READ)
                        attend(u - 1, 1 - p, [0])
                    if j == AJ + 1 and not first:
                        attend(u - 1, 1 - p, [1, 2, 3])
                    if j == VJ and not last:
                        project_v(u + 1, *following)
                    if j == YJ and not first:
                        project_out(u - 1, 1 - p)

            attention_units(pe, attention)
            u = UNITS - 1
            for j in range(BLK - LAG, BLK):
                transpose(u, 1, j)
            attend(u, 1, [0, 1, 2, 3])
            project_out(u, 1)

            transpose_x1(B - 1, UNITS)
            logits(B - 1)
            pe.wait_ge(routed, ROUTE * (B - 1) + LOGITS_READ)
            rank(B - 1, UNITS)

            def transpose_x(t, s):
                p = s % 2
                pe.wait_ge(xt_in[s], 16 * (t // XT + 1))
                nc.tensor.transpose(XB[p][:, 0:P], xt[s][:, 0:C], ident[:, :]).then_inc(x_tr, 1)

            def up(t, s):
                p = s % 2
                pe.wait_ge(w_ready, t + 1)
                pe.wait_ge(xT_ready, t + 1)
                for ib in range(IB):
                    last = nc.tensor.matmul(HB[p][:, ib * P:ib * P + P], w_tile[p][:, ib * P:ib * P + P], xT[p][:, :],
                                            start=True, stop=True)
                last.then_inc(up_done, 1)

            def down(t, s, e):
                p = s % 2
                pe.wait_ge(gelu_done, t + 1)
                wait(pe, y_ready, t - 1)
                for ib in range(IB):
                    last = nc.tensor.matmul(FB[p][:, 0:C], hT[p][:, ib * P:ib * P + P],
                                            wdown[:, bass.ds(e * IB + ib, 1), :].rearrange("p a c -> p (a c)"),
                                            start=(ib == 0), stop=(ib == IB - 1))
                last.then_inc(down_done, 1)

            def expert(t):
                return pe.value_load(tile_expert[0:1, bass.ds(t, 1)], min_val=0, max_val=E - 1)

            def ffn(t, s, first, last):
                if first:
                    pe.wait_ge(tables_ready, 1)
                    pe.wait_ge(w_in, 32)
                    pe.wait_ge(routed, ROUTE * B)
                    pe.wait_ge(y_added, UNITS)
                    pe.wait_ge(v_ready, UNITS)
                    transpose_x(0, 0)
                e = None if first else expert(t - 1)
                if not last:
                    transpose_x(t + 1, (s + 1) % XT)
                up(t, s)
                if not first:
                    down(t - 1, (s - 1) % XT, e)

            tiles(pe, ffn)
            down(TILES - 1, XT - 1, expert(TILES - 1))

        @block.scalar
        def _(act):
            def copy_v(u, p, bank=AB):
                act.wait_ge(v_proj, u + 1)
                nc.scalar.activation(V[p][:, :, :], bank[:, :].rearrange("k (b f) -> k b f", b=QB), ACT.Copy).then_inc(v_ready, 1)

            def exp(u, p, j):
                g, qb = BLK * u + j, ORDER[j][1]
                act.wait_ge(maxed, g + 1)
                wait(act, transposed, g - BLK + 1)
                n = (qb + 1) * P
                nc.scalar.activation(Pr[j][:, 0:n], Sm[j % 4][:, 0:n], ACT.Exp, bias=nmax[:, j:j + 1], scale=-1.0,
                                     accum_out=rsum[:, j:j + 1]).then_inc(exped, 1)

            def copy_pt(u, p, j):
                h, qb = ORDER[j]
                act.wait_ge(transposed, BLK * u + j + 1)
                nc.scalar.activation(PT[p][:, h, 0:qb + 1, qb * P:qb * P + P],
                                     TB[j % 2][:, 0:(qb + 1) * P].rearrange("k (b q) -> k b q", q=P),
                                     ACT.Copy).then_inc(pt_ready, 1)

            def copy_o(u, p):
                act.wait_ge(pv_done, u + 1)
                nc.scalar.activation(OT[p][:, :], OB[:, :], ACT.Copy).then_inc(o_ready, 1)

            def root(b):
                act.wait_ge(eps_set, 1)
                act.wait_ge(routed, ROUTE * b + VAR)
                nc.scalar.activation(sd[:, :], mv[:, :, 1], ACT.Sqrt, bias=eps_t[:, 0:1]).then_inc(sd_ready, 1)

            def copy_x1T(b):
                act.wait_ge(x1_tr, b + 1)
                nc.scalar.activation(x1T[:, :], OB[:, :], ACT.Copy).then_inc(x1T_ready, 1)

            def copy_rows(b):
                act.wait_ge(routed, ROUTE * b + X1)
                nc.scalar.activation(pay[:, :, 1, 0:C], pay[:, :, 0, 0:C], ACT.Copy).then_inc(pay_ready, 1)
                nc.scalar.activation(x_acc[:, bass.ds(b * QB, QB), :], pay[:, :, 0, 0:C], ACT.Copy).then_inc(x1_kept, 1)

            def exp_logits(b):
                act.wait_ge(routed, ROUTE * b + SHIFTED)
                nc.scalar.activation(wt[:, :, :], lg[:, :, :], ACT.Exp).then_inc(gate_exp, 1)

            def attention(u, p, n, batch, first, last):
                route = n is not None and not (isinstance(batch, int) and batch == 0)
                if first:
                    copy_v(0, 0, SB[3])
                for j in range(BLK):
                    if j == AJ + 2 and not first:
                        copy_o(u - 1, 1 - p)
                    if j == VJ + 1 and not last:
                        copy_v(u + 1, 1 - p)
                    if route and (n, j) == (3, 2):
                        copy_x1T(batch - 1)
                    if j >= LAG:
                        copy_pt(u, p, j - LAG)
                    elif not first:
                        copy_pt(u - 1, 1 - p, BLK + j - LAG)
                    exp(u, p, j)
                    if n == PAIRS - 2 and not last_batch(batch):
                        if j == KJ + 2:
                            act.wait_ge(x_next_in, 16 * (batch + 1))
                            act.wait_ge(k_proj, u + 2)
                            nc.scalar.activation(x_hi[:, :], x_next[:, :], ACT.Copy).then_inc(x_high, 1)
                        if j == VJ + 2:
                            act.wait_ge(v_proj, u + 2)
                            nc.scalar.activation(x_cur[:, :], x_next[:, :], ACT.Copy).then_inc(x_moved, 1)
                    if route and (n, j) == ROOT_AT:
                        root(batch - 1)
                    if route and (n, j) == (3, 6):
                        exp_logits(batch - 1)
                    if route and (n, j) == (3, 0):
                        copy_rows(batch - 1)

            attention_units(act, attention)
            u = UNITS - 1
            for j in range(BLK - LAG, BLK):
                copy_pt(u, 1, j)
            copy_o(u, 1)
            nc.scalar.activation(warm[:, :], eps_t[:, :], ACT.Sqrt)
            root(B - 1)
            copy_x1T(B - 1)
            exp_logits(B - 1)
            copy_rows(B - 1)

            nc.scalar.activation(warm[:, :], eps_t[:, :], ACT.Gelu)

            def copy_xT(t, s):
                act.wait_ge(x_tr, t + 1)
                nc.scalar.activation(xT[s % 2][:, :], XB[s % 2][:, 0:P], ACT.Copy).then_inc(xT_ready, 1)

            def ffn(t, s, first, last):
                if first:
                    copy_xT(0, 0)
                if not last:
                    copy_xT(t + 1, s + 1)
                act.wait_ge(up_done, t + 1)
                nc.scalar.activation(hT[s % 2][:, :], HB[s % 2][:, :], ACT.Gelu).then_inc(gelu_done, 1)

            tiles(act, ffn)
            def root2_of(n, b):
                of = slice(QB * b, QB * b + QB)
                act.wait_ge(var2, gathered(n, b))
                nc.scalar.activation(sd2[:, n, of], mv2[:, n, of, 1], ACT.Sqrt, bias=eps_t[:, 0:1]).then_inc(root2, 1)

            def norm2_of(n, b):
                act.wait_ge(factors_ready, scaled(n, b))
                for i in range(QB * b, QB * b + QB - n):
                    last = nc.scalar.activation(f_acc[:, i, :], f_acc[:, i, :], ACT.Identity,
                                                bias=shift2[:, n, i:i + 1], scale=rstd2[:, n, i:i + 1])
                last.then_inc(normed2, 1)

            for k in range(B + 2):
                if k < B:
                    root2_of(0, k)
                if k >= 2:
                    norm2_of(1, k - 2)
                if k < B:
                    norm2_of(0, k)
                if 1 <= k <= B:
                    root2_of(1, k - 1)

        @block.vector
        def _(dve):
            steps = [0]

            def done(ins):
                steps[0] += 1
                ins.then_inc(chain, 1)
                dve.wait_ge(chain, steps[0])

            swap = [i ^ 1 for i in range(32)]

            def rope_q(u):
                dve.wait_ge(q_proj, u + 1)
                wait(dve, q_ready, u)
                nc.vector.tensor_tensor(q_cos[:, :], AB[:, :], cos_t[:, :], ALU.mult)
                nc.vector.stream_shuffle(q_rot[:, :], AB[:, :], swap).then_inc(q_read, 1)

            def rope_k(u):
                dve.wait_ge(k_proj, u + 1)
                wait(dve, k_ready, 2 * u)
                nc.vector.tensor_tensor(k_cos[:, :], AB[:, :], cos_t[:, :], ALU.mult)
                nc.vector.stream_shuffle(k_rot[:, :], AB[:, :], swap).then_inc(k_read, 1)

            def first_k():
                dve.wait_ge(k_proj, 1)
                nc.vector.tensor_tensor(k_cos[:, :], SB[2][:, :], cos_t[:, :], ALU.mult)
                nc.vector.stream_shuffle(k_rot[:, :], SB[2][:, :], swap).then_inc(k_read, 1)
                dve.wait_ge(k_read, 1)
                nc.vector.tensor_tensor(k_rot[:, :], k_rot[:, :], sin_t[:, :], ALU.mult).then_inc(k_mul, 1)
                dve.wait_ge(k_mul, 1)
                dve.wait_ge(pool_set, POOL_SET)
                for h in range(2):
                    half = slice(D * h, D * h + D)
                    nc.vector.tensor_tensor(kM[0][half, h, :], k_cos[half, :], k_rot[half, :], ALU.add).then_inc(k_ready, 1)

            def mask_max(u, j):
                n = (ORDER[j][1] + 1) * P
                nc.vector.tensor_tensor_reduce(out=Sm[j % 4][:, 0:n], in0=SB[j % 4][:, 0:n], in1=causal[:, T - n:T],
                                               scale=-0.125, scalar=HUGE, op0=ALU.add, op1=ALU.min,
                                               accum_out=nmax[:, j:j + 1]).then_inc(maxed, 1)

            def invert(u, j):
                dve.wait_ge(exped, BLK * u + j + 1)
                nc.vector.reciprocal(rinv[:, j:j + 1], rsum[:, j:j + 1]).then_inc(inverted, 1)

            def norm(u, j):
                n = (ORDER[j][1] + 1) * P
                dve.wait_ge(inverted, BLK * u + j + 1)
                nc.vector.tensor_scalar(Pr[j][:, 0:n], Pr[j][:, 0:n], rinv[:, j:j + 1], None,
                                        ALU.mult).then_inc(normed, 1)

            def add_y(u):
                b = u // PAIRS
                tiles = x_acc[:, bass.ds(b * QB, QB), :]
                if isinstance(u, int) and u == 0:
                    dve.wait_ge(x_set, QB)
                dve.wait_ge(y_done, u + 1)
                wait(dve, y_added, u)
                nc.vector.tensor_tensor(tiles, OB[:, :].rearrange("t (b c) -> t b c", b=QB), tiles,
                                        ALU.add).then_inc(y_added, 1)

            def over_e(t):
                return t[:, :].unsqueeze(2).to_broadcast([P, QB, E])

            def over_t(t):
                return t[:, :].unsqueeze(1).to_broadcast([P, QB, E])

            def stats(b, tiles_):
                for i in tiles_:
                    last = nc.vector.bn_stats(st[:, i, :], x_tile(b, i))
                return last

            def sum_stats(b):
                for i in range(QB):
                    last = nc.vector.bn_aggr(mv[:, i, :], st[:, i, :])
                return last

            def norm_x1(b):
                for i in range(QB):
                    last = nc.vector.tensor_scalar(pay[:, i, 0, 0:C], x_tile(b, i), mv[:, i, 0:1], rstd[:, i:i + 1],
                                                   ALU.subtract, ALU.mult)
                return last

            def pick(weights, best, chosen):
                return [
                    lambda b: nc.vector.tensor_reduce(best[:, :], weights[:, :, :], AX.X, ALU.max),
                    lambda b: nc.vector.tensor_tensor(chosen[:, :, :], weights[:, :, :], over_e(best), ALU.is_equal),
                    lambda b: nc.vector.tensor_tensor(chosen[:, :, :], chosen[:, :, :], over_t(order), ALU.mult),
                    lambda b: nc.vector.tensor_reduce(s1[:, :], chosen[:, :, :], AX.X, ALU.max),
                    lambda b: nc.vector.tensor_tensor(chosen[:, :, :], chosen[:, :, :], over_e(s1), ALU.is_equal),
                ]

            def choose(b):
                nc.vector.tensor_tensor(cc[:, :, :], c1[:, :, :], c2[:, :, :], ALU.add)
                return nc.vector.scalar_tensor_tensor(out=den[:, :], in0=m1[:, :], scalar=GATE_EPS, in1=m2[:, :],
                                                      op0=ALU.add, op1=ALU.add)

            def row_weights(b):
                nc.vector.tensor_tensor(pay[:, :, 0, C], m1[:, :], den[:, :], ALU.mult)
                return nc.vector.tensor_tensor(pay[:, :, 1, C], m2[:, :], den[:, :], ALU.mult)

            def ahead(i):
                return lambda b: nc.vector.tensor_tensor(before_n[:, i, :], before_n[:, i - 1, :], ranks[:, QB + i - 1, :], ALU.add)

            def place_rows(b):
                nc.vector.tensor_tensor(next_row[:, :], before_n[:, QB - 1, :], ranks[:, 2 * QB - 1, :], ALU.add)
                return nc.vector.tensor_tensor(slots_f[:, :, :], before_n[:, :, :], ranks[:, 0:QB, :], ALU.add)

            def mask_slots(b):
                nc.vector.tensor_tensor(c1[:, :, :], c1[:, :, :], slots_f[:, :, :], ALU.mult)
                return nc.vector.tensor_tensor(c2[:, :, :], c2[:, :, :], slots_f[:, :, :], ALU.mult)

            def sum_slots(b):
                nc.vector.tensor_reduce(slot_f[:, :, 0], c1[:, :, :], AX.X, ALU.add)
                return nc.vector.tensor_reduce(slot_f[:, :, 1], c2[:, :, :], AX.X, ALU.add)

            def write_slots(b):
                nc.vector.tensor_copy(pay[:, :, :, C + 1], row_id[:, bass.ds(b * QB, QB), :])
                return nc.vector.tensor_copy(slot[:, :, :], slot_f[:, :, :])

            route_steps = [
                ((1, 5, 0), lambda b: [(y_added, PAIRS * (b + 1))], lambda b: stats(b, (0, 1))),
                ((1, 6, 0), None, lambda b: stats(b, (2, 3))),
                ((1, 7, 0), None, sum_stats),
                ((2, 5, 0), lambda b: [(sd_ready, b + 1)], lambda b: nc.vector.reciprocal(rstd[:, :], sd[:, :])),
                ((2, 6, 1), lambda b: [(rows_sent, 16 * QB * K * b)], norm_x1),
                ((3, 4, 0), lambda b: [(logits_done, b + 1)], lambda b: nc.vector.tensor_tensor(
                    lg[:, :, :], OB[:, 0:QB * E].rearrange("p (n e) -> p n e", e=E), over_t(ebias_t), ALU.add)),
                ((3, 4, 1), None, lambda b: nc.vector.tensor_reduce(m1[:, :], lg[:, :, :], AX.X, ALU.max)),
                ((3, 5, 0), None, lambda b: nc.vector.tensor_tensor(lg[:, :, :], lg[:, :, :], over_e(m1), ALU.subtract)),
                ((3, 7, 1), lambda b: [(gate_exp, b + 1)],
                 lambda b: nc.vector.tensor_reduce(s1[:, :], wt[:, :, :], AX.X, ALU.add)),
                ((4, 0, 0), None, lambda b: nc.vector.reciprocal(s1[:, :], s1[:, :])),
                ((4, 0, 1), None, lambda b: nc.vector.tensor_tensor(wt[:, :, :], wt[:, :, :], over_e(s1), ALU.mult)),
            ] + [((4, 1 + i // 2, i % 2), None, step) for i, step in enumerate(pick(wt, m1, c1))] + [
                ((4, 3, 1), None, lambda b: nc.vector.scalar_tensor_tensor(
                    out=w2[:, :, :], in0=c1[:, :, :], scalar=-2.0, in1=wt[:, :, :], op0=ALU.mult, op1=ALU.add)),
            ] + [((4, 4 + i // 2, i % 2), None, step) for i, step in enumerate(pick(w2, m2, c2))] + [
                ((4, 6, 1), None, choose),
                ((4, 7, 0), None, lambda b: nc.vector.reciprocal(den[:, :], den[:, :])),
                ((4, 7, 1), None, row_weights),
                ((5, 3, 0), lambda b: [(ranked, b + 1)], lambda b: nc.vector.tensor_copy(
                    ranks[:, :, :], OB[:, 0:2 * QB * E].rearrange("p (n e) -> p n e", e=E))),
                ((5, 3, 1), None, lambda b: nc.vector.tensor_copy(before_n[:, 0, :], next_row[:, :])),
                ((5, 4, 0), None, ahead(1)),
                ((5, 4, 1), None, ahead(2)),
                ((5, 5, 0), None, ahead(3)),
                ((5, 5, 1), None, place_rows),
                ((5, 6, 0), None, mask_slots),
                ((5, 6, 1), None, sum_slots),
                ((5, 7, 0), None, write_slots),
            ]
            assert len(route_steps) == ROUTE

            def route_step(b, place):
                for i, (at, needs, step) in enumerate(route_steps):
                    if place is None or at == place:
                        wait(dve, routed, ROUTE * b + i)
                        for semaphore, count in needs(b) if needs else []:
                            wait(dve, semaphore, count)
                        if i < VAR:
                            dve.sem_inc(stats_turn, 1)
                        step(b).then_inc(routed, 1)

            def attention(u, p, n, batch, first, last):
                route = n is not None and not (isinstance(batch, int) and batch == 0)
                if first:
                    dve.wait_ge(consts_in, 16 * 5)
                    rope_q(0)
                    first_k()
                    nc.vector.memset(eps_t[:, :], LN_EPS).then_inc(eps_set, 1)
                    dve.wait_ge(pool_set, POOL_SET)
                for j in range(BLK):
                    if j == 0 and not (isinstance(u, int) and u < 2):
                        add_y(u - 2)
                    if j == QJ + 1 and not last:
                        rope_q(u + 1)
                    if j == KJ + 1 and not last:
                        rope_k(u + 1)
                    if route:
                        route_step(batch - 1, (n, j, 0))
                    before = (u, j - 2) if j >= 2 else None if first else (u - 1, BLK + j - 2)
                    dve.wait_ge(scored, BLK * u + j + 1)
                    if before:
                        invert(*before)
                    mask_max(u, j)
                    if before:
                        norm(*before)
                    if n == PAIRS - 2 and not last_batch(batch) and j == KJ + 3:
                        dve.wait_ge(x_high, batch + 1)
                        nc.vector.tensor_tensor(x_lo[:, :], x_next[:, :], x_hi[:, :], ALU.subtract).then_inc(x_split, 1)
                    if isinstance(u, int) and u == 1 and 0 < j <= QB:
                        dve.wait_ge(x_in, 16)
                        part = x_acc[:, (j - 1) * NT // QB:j * NT // QB, :]
                        nc.vector.tensor_tensor(part, part, bo_t[:, :].unsqueeze(1).to_broadcast([P, NT // QB, C]),
                                                ALU.add).then_inc(x_set, 1)
                    if route:
                        route_step(batch - 1, (n, j, 1))

            attention_units(dve, attention)
            for j in (BLK - 2, BLK - 1):
                invert(UNITS - 1, j)
                norm(UNITS - 1, j)
            add_y(UNITS - 2)
            add_y(UNITS - 1)
            dve.wait_ge(y_added, UNITS)
            route_step(B - 1, None)
            dve.wait_ge(routed, ROUTE * B)

            nc.vector.tensor_copy(pad_at[:, :], next_row[0:1, :]).then_inc(pads_ready, 1)
            done(nc.vector.tensor_tensor(count[:, :], next_row[:, :], region[:, :], ALU.subtract))
            done(nc.vector.tensor_scalar(tiles_of[:, :], count[:, :], 1.0 / P, (P / 2 - 0.5) / P, ALU.mult, ALU.add))
            done(nc.vector.tensor_scalar(tiles_of[:, :], tiles_of[:, :], MAGIC, None, ALU.add))
            done(nc.vector.tensor_scalar(tiles_of[:, :], tiles_of[:, :], -MAGIC, None, ALU.add))
            done(nc.vector.memset(start[:, :], 0.0))
            done(nc.vector.tensor_copy(sums[0][:, :], tiles_of[:, :]))
            for n, k in enumerate((1, 2, 4)):
                src, dst = sums[n % 2], (sums[1] if n % 2 == 0 else sums[0]) if k < 4 else start[:, 1:E + 1]
                nc.vector.tensor_copy(dst[:, 0:k], src[:, 0:k])
                done(nc.vector.tensor_tensor(dst[:, k:E], src[:, k:E], src[:, 0:E - k], ALU.add))

            def by_expert(t):
                return t[0:1, 0:E].unsqueeze(1).to_broadcast([1, TILES, E])

            def by_tile(t):
                return t[0:1, :].unsqueeze(2).to_broadcast([1, TILES, E])

            done(nc.vector.tensor_tensor(past[:, :, :], by_tile(tile_no), by_expert(start), ALU.is_ge))
            done(nc.vector.tensor_reduce(exp_f[:, :], past[:, :, :], AX.X, ALU.add))
            done(nc.vector.tensor_scalar(exp_f[:, :], exp_f[:, :], -1.0, None, ALU.add))
            nc.vector.tensor_copy(tile_expert[:, :], exp_f[:, :])
            done(nc.vector.tensor_tensor(past[:, :, :], past[:, :, :], by_expert(start), ALU.mult))
            done(nc.vector.tensor_reduce(row_f[:, :], past[:, :, :], AX.X, ALU.max))
            done(nc.vector.tensor_tensor(row_f[:, :], tile_no[:, :], row_f[:, :], ALU.subtract))
            done(nc.vector.tensor_scalar(row_f[:, :], row_f[:, :], float(P), float(-SPARE), ALU.mult, ALU.add))
            done(nc.vector.scalar_tensor_tensor(out=row_f[:, :], in0=exp_f[:, :], scalar=float(REGION), in1=row_f[:, :],
                                                op0=ALU.mult, op1=ALU.add))
            done(nc.vector.tensor_scalar(ok_f[:, :], tile_no[:, :], start[0:1, E:E + 1], None, ALU.is_lt))
            done(nc.vector.tensor_tensor(row_f[:, :], row_f[:, :], ok_f[:, :], ALU.mult))
            done(nc.vector.tensor_scalar(row_f[:, :], row_f[:, :], float(SPARE), None, ALU.add))
            nc.vector.tensor_copy(tile_row[:, :], row_f[:, :]).then_inc(tables_ready, 1)

            def take_meta(t, s):
                wait(dve, ys_sent[s], 16 * (t // XT))
                dve.wait_ge(xt_in[s], 16 * (t // XT + 1))
                nc.vector.tensor_tensor(y_row[s][:, :], xt[s][:, C + 1:C + 2], pad_id[:, bass.ds(t, 1)], ALU.max)
                nc.vector.tensor_copy(y_weight[s][:, :], xt[s][:, C:C + 1]).then_inc(meta_taken, 1)

            def take_expert(t, s):
                e = dve.value_load(tile_expert[0:1, bass.ds(t, 1)], min_val=0, max_val=E - 1)
                wait(dve, up_done, t - 1)
                nc.vector.tensor_copy(w_tile[s % 2][:, :], wup[:, bass.ds(e * I, I)]).then_inc(w_ready, 1)

            def ffn(t, s, first, last):
                if first:
                    dve.wait_ge(tables_ready, 1)
                    dve.wait_ge(w_in, 32)
                    take_expert(0, 0)
                if not last:
                    take_expert(t + 1, (s + 1) % XT)
                take_meta(t, s)
                if not first:
                    weight_y(t - 1, (s - 1) % XT)

            def weight_y(t, s):
                dve.wait_ge(meta_taken, t + 1)
                dve.wait_ge(down_done, t + 1)
                nc.vector.tensor_scalar(ys[s][:, :], FB[s % 2][:, 0:C], y_weight[s][:, :], None, ALU.mult).then_inc(y_ready, 1)

            tiles(dve, ffn)
            weight_y(TILES - 1, XT - 1)

            def gather_stats(n, b, tiles_=range(QB)):
                for i in tiles_:
                    last = nc.vector.bn_stats(st2[:, n, QB * b + i, :], f_acc[:, QB * b + i, :])
                if i == QB - 1:
                    last.then_inc(stats_in, 1)

            def sum_stats2(n, b):
                dve.wait_ge(stats_in, gathered(n, b))
                for i in range(QB * b, QB * b + QB):
                    last = nc.vector.bn_aggr(mv2[:, n, i, :], st2[:, n, i, :])
                last.then_inc(var2, 1)

            def invert_root(n, b):
                of = slice(QB * b, QB * b + QB)
                dve.wait_ge(root2, gathered(n, b))
                nc.vector.reciprocal(rstd2[:, n, of], sd2[:, n, of]).then_inc(root_inverted, 1)

            def shift(n, b):
                of = slice(QB * b, QB * b + QB)
                dve.wait_ge(root_inverted, scaled(n, b))
                nc.vector.scalar_tensor_tensor(out=shift2[:, n, of], in0=mv2[:, n, of, 0], scalar=-1.0,
                                               in1=rstd2[:, n, of], op0=ALU.mult, op1=ALU.mult).then_inc(factors_ready, 1)

            def twice_x1(b):
                part = f_acc[:, QB * b:QB * b + QB, :]
                dve.wait_ge(normed2, scaled(0, b))
                nc.vector.scalar_tensor_tensor(out=part, in0=x_acc[:, QB * b:QB * b + QB, :], scalar=2.0, in1=part,
                                               op0=ALU.mult, op1=ALU.add).then_inc(x1_twice, 1)

            dve.wait_ge(x1_kept, B)
            for k in range(B + 2):
                if k < B:
                    dve.wait_ge(y_summed, k + 1)
                    gather_stats(0, k)
                if k < B:
                    sum_stats2(0, k)
                if k >= 2:
                    invert_root(1, k - 2)
                if k >= 2:
                    shift(1, k - 2)
                if 1 <= k <= B:
                    twice_x1(k - 1)
                if k < B:
                    invert_root(0, k)
                if 1 <= k <= B:
                    dve.wait_ge(x1_twice, k)
                    gather_stats(1, k - 1, (0, 1))
                if k < B:
                    shift(0, k)
                if 1 <= k <= B:
                    gather_stats(1, k - 1, (2, 3))
                if 1 <= k <= B:
                    sum_stats2(1, k - 1)


def rope_tables():
    import numpy as np
    inv_freq = (np.float32(1.0) / np.float32(10000.0) ** (np.arange(0, D, 2, dtype=np.float32) / np.float32(D))).astype(np.float32)
    ang = (np.arange(T, dtype=np.float32)[None, :] * inv_freq[:, None]).astype(np.float32)
    sign = np.array([-1.0, 1.0], np.float32)[:, None]
    cos = np.tile(np.repeat(np.cos(ang), 2, axis=0), (2, 1))
    sin = np.tile((np.sin(ang)[:, None, :] * sign).reshape(D, T), (2, 1))
    return np.ascontiguousarray(cos, np.float32), np.ascontiguousarray(sin, np.float32)


def kernel(**inputs):
    import numpy as np
    import concourse.bacc as bacc
    from concourse.bass_utils import run_bass_kernel_spmd

    a = {k.replace("L0_", ""): np.asarray(v) for k, v in inputs.items()}
    cos, sin = rope_tables()
    x = a["attn_x"].reshape(B * T, C)
    wqk = np.stack([a[f"attn_W{n}"].reshape(C, PAIRS, P) for n in "qk"], axis=2)
    arrays = {
        "xT": x.T,
        "x": x,
        "wqk": wqk.reshape(C, PAIRS * 2 * P),
        "wv": a["attn_Wv"],
        "wo": a["attn_Wo"],
        "bo": np.broadcast_to(a["attn_bo"], (P, C)),
        "cos": cos,
        "sin": sin,
        "gate": a["ffn_gate_w"].T,
        "ebias": np.broadcast_to(a["ffn_expert_bias"], (P, E)),
        "wup": a["ffn_w_up"].reshape(E * I, C).T,
        "wdown": a["ffn_w_down"].reshape(E, C, IB, P).transpose(3, 0, 2, 1).reshape(P, E * IB, C),
    }
    arrays = {f"in_{k}": np.ascontiguousarray(v) for k, v in arrays.items()}
    nc = bacc.Bacc("TRN2", target_bir_lowering=False, num_devices=1)
    args = [nc.dram_tensor(k, v.shape, mybir.dt.from_np(v.dtype), kind="ExternalInput").ap() for k, v in arrays.items()]
    args.append(nc.dram_tensor("xrows", (SPARE + P, ROW), F32, kind="Internal").ap())
    args.append(nc.dram_tensor("yrows", (Y0 + B * T * K, C), F32, kind="Internal").ap())
    out = nc.dram_tensor("out_0", (B * T, C), F32, kind="ExternalOutput").ap()
    build_block(nc, *args, out)
    r = run_bass_kernel_spmd(nc, [arrays], core_ids=[0])
    return r.results[0]["out_0"].reshape(B, T, C)
```
